# Optimizing a Trainium2 kernel written in Bass

```python
import numpy as np
import jax
import jax.numpy as jnp

def _softmax(x, axis=-1):
    return jax.nn.softmax(x, axis=axis)

def _gelu(x):
    return jax.nn.gelu(x, approximate=True)

def _silu(x):
    return jax.nn.silu(x)

def _sigmoid(x):
    return jax.nn.sigmoid(x)

def _layernorm(x, axis=-1, eps=1e-05):
    m = jnp.mean(x, axis=axis, keepdims=True)
    v = jnp.var(x, axis=axis, keepdims=True)
    return (x - m) / jnp.sqrt(v + eps)

def _scatter_add(tgt, idx, src, axis=0):
    return tgt.at[idx].add(src)

def _segment_sum(src, seg, n):
    return jax.ops.segment_sum(src, seg, n)
kernel_name = 'mk_flamingo_gated_d2_seqx_r4_8ea228'

def setup_inputs(seed: int=0):
    np.random.seed(seed)
    _w = jnp.asarray

    def _rec_inputs():
        import jax
        import jax.numpy as jnp
        _rk = jax.random.key(seed)
        x = 7.22e-05 + 1 * jax.random.normal(jax.random.fold_in(_rk, 1), (32, 128, 256), jnp.float32)
        _lenS = 128 - jax.random.randint(jax.random.fold_in(_rk, 7), (32,), 0, max(1, 128 // 4) + 1, jnp.int32)
        _lenS2 = 128 - jax.random.randint(jax.random.fold_in(_rk, 8), (32,), 0, max(1, 128 // 4) + 1, jnp.int32)
        _ctx_1024P = jax.random.normal(jax.random.fold_in(_rk, 11), (32, 16, 256), jnp.float32)
        _ctx_1024c = jax.random.dirichlet(jax.random.fold_in(_rk, 511), 0.3 * jnp.ones((16,), jnp.float32), (32, 128))
        _ctx_1024t = jnp.einsum('bsk,bkd->bsd', _ctx_1024c, _ctx_1024P)
        _ctx_1024t = _ctx_1024t * jax.lax.rsqrt(jnp.mean(jnp.square(_ctx_1024t)) + 1e-12) * 0.953939
        ctx_1024 = 4.13588e-05 + 0.999923 * (_ctx_1024t + 0.3 * jax.random.normal(jax.random.fold_in(_rk, 611), (32, 128, 256), jnp.float32))
        _validS = jnp.arange(128)[None, :] < _lenS[:, None]
        _validS2 = jnp.arange(128)[None, :] < _lenS2[:, None]
        _causal = jnp.tril(jnp.ones((128, 128), dtype=bool))
        mask_BxSxS2_fk0 = jnp.where(jnp.broadcast_to(_validS2[:, None, :], (32, 128, 128)), 0.0, 1.0).astype(jnp.float32)
        _g = jax.random.normal(jax.random.fold_in(_rk, 9001), (2, 2), jnp.float32)
        _g = jnp.sign(_g) * jnp.maximum(jnp.abs(_g), 1.0) + (_g == 0) * 1.0
        g_xattn = _g[0]
        g_ffn = _g[1]
        return (x, ctx_1024, mask_BxSxS2_fk0, g_xattn, g_ffn)
    x, ctx_1024, mask_BxSxS2_fk0, g_xattn, g_ffn = _rec_inputs()

    def _L0_xattn_setup():
        import jax, jax.numpy as jnp
        import numpy as np
        H = 16
        DK = 64
        D_MODEL = 256
        key = jax.random.key(seed)
        ks = jax.random.split(key, 9)
        B, T, D = (4, 512, D_MODEL)
        scale = 1.0 / np.sqrt(D)
        return {'Q': jax.random.normal(ks[0], (B, T, D), dtype=jnp.float32), 'K': jax.random.normal(ks[1], (B, T, D), dtype=jnp.float32), 'V': jax.random.normal(ks[2], (B, T, D), dtype=jnp.float32), 'Wq': jax.random.normal(ks[3], (D, D), dtype=jnp.float32) * scale, 'bq': jax.random.normal(ks[4], (D,), dtype=jnp.float32) * scale, 'Wk': jax.random.normal(ks[5], (D, D), dtype=jnp.float32) * scale, 'bk': jax.random.normal(ks[6], (D,), dtype=jnp.float32) * scale, 'Wv': jax.random.normal(ks[7], (D, D), dtype=jnp.float32) * scale, 'bv': jax.random.normal(ks[8], (D,), dtype=jnp.float32) * scale}
    _L0_xattn_all = _L0_xattn_setup()
    _L0_xattn_in = {k: v for k, v in _L0_xattn_all.items() if k in ('Wq', 'bq', 'Wk', 'bk', 'Wv', 'bv')}
    del _L0_xattn_all

    def _L0_ffn_setup():
        import jax, jax.numpy as jnp
        import numpy as np
        EPS = 1e-08

        def _ste(x, q):
            return x + jax.lax.stop_gradient(q - x)

        def quant_act_uint8(x):
            s = jax.lax.stop_gradient(jnp.maximum(jnp.max(x), EPS)) / 255.0
            q = jnp.clip(jnp.round(x / s), 0.0, 255.0) * s
            return (_ste(x, q), s)

        def quant_weight_int8_perchannel(w):
            s = jax.lax.stop_gradient(jnp.maximum(jnp.max(jnp.abs(w), axis=1, keepdims=True), EPS)) / 127.0
            q = jnp.clip(jnp.round(w / s), -128.0, 127.0) * s
            return (_ste(w, q), s[:, 0])

        def quant_bias_int32(b, s_in, s_w):
            s = jax.lax.stop_gradient(s_in * s_w)
            q = jnp.round(b / s) * s
            return _ste(b, q)

        def quant_linear(x, w, b):
            xq, s_in = quant_act_uint8(x)
            wq, s_w = quant_weight_int8_perchannel(w)
            bq = quant_bias_int32(b, s_in, s_w)
            return jnp.einsum('btd,fd->btf', xq, wq) + bq
        key = jax.random.key(seed)
        k1, k2, k3, k4, k5 = jax.random.split(key, 5)
        B, S, D, F = (4, 512, 256, 1024)
        return {'x': jax.random.normal(k1, (B, S, D), dtype=jnp.float32), 'w1': jax.random.normal(k2, (F, D), dtype=jnp.float32) * (1.0 / np.sqrt(D)), 'b1': jax.random.normal(k3, (F,), dtype=jnp.float32) * 0.01, 'w2': jax.random.normal(k4, (D, F), dtype=jnp.float32) * (1.0 / np.sqrt(F)), 'b2': jax.random.normal(k5, (D,), dtype=jnp.float32) * 0.01}
    _L0_ffn_all = _L0_ffn_setup()
    _L0_ffn_in = {k: v for k, v in _L0_ffn_all.items() if k in ('w1', 'b1', 'w2', 'b2')}
    del _L0_ffn_all

    def _L1_xattn_setup():
        import jax, jax.numpy as jnp
        import numpy as np
        INPUT_DIM, ATTN_DIM, OUTPUT_DIM = (256, 256, 256)
        B, LQ, LKV = (4, 512, 512)
        key = jax.random.key(seed)
        ks = jax.random.split(key, 10)
        s = 1.0 / np.sqrt(INPUT_DIM)
        return {'primary': jax.random.normal(ks[0], (B, LQ, INPUT_DIM), jnp.float32), 'context_sequence': jax.random.normal(ks[1], (B, LKV, INPUT_DIM), jnp.float32), 'mask': jax.random.randint(ks[2], (B, LQ, LKV), 0, 2).astype(jnp.float32), 'Wq': jax.random.uniform(ks[3], (INPUT_DIM, ATTN_DIM), jnp.float32, -s, s), 'bq': jax.random.uniform(ks[4], (ATTN_DIM,), jnp.float32, -s, s), 'Wk': jax.random.uniform(ks[5], (INPUT_DIM, ATTN_DIM), jnp.float32, -s, s), 'bk': jax.random.uniform(ks[6], (ATTN_DIM,), jnp.float32, -s, s), 'Wv': jax.random.uniform(ks[7], (INPUT_DIM, OUTPUT_DIM), jnp.float32, -s, s), 'bv': jax.random.uniform(ks[8], (OUTPUT_DIM,), jnp.float32, -s, s)}
    _L1_xattn_all = _L1_xattn_setup()
    _L1_xattn_in = {k: v for k, v in _L1_xattn_all.items() if k in ('Wq', 'bq', 'Wk', 'bk', 'Wv', 'bv')}
    del _L1_xattn_all

    def _L1_ffn_setup():
        import jax, jax.numpy as jnp
        import numpy as np
        H = 256
        I = 512
        E = 8
        TOP_K = 2
        NUM_SHARED = 1
        key = jax.random.key(seed)
        ks = jax.random.split(key, 9)
        s = 0.02
        x = jax.random.normal(ks[0], (2, 512, H), dtype=jnp.float32)
        sg_w = jax.random.normal(ks[1], (I, H), dtype=jnp.float32) * s
        su_w = jax.random.normal(ks[2], (I, H), dtype=jnp.float32) * s
        sd_w = jax.random.normal(ks[3], (H, I), dtype=jnp.float32) * s
        router_w = jax.random.normal(ks[4], (E, H), dtype=jnp.float32) * s
        routing_bias = jnp.zeros((E,), dtype=jnp.float32)
        wg = jax.random.normal(ks[5], (E, I, H), dtype=jnp.float32) * s
        wu = jax.random.normal(ks[6], (E, I, H), dtype=jnp.float32) * s
        wd = jax.random.normal(ks[7], (E, H, I), dtype=jnp.float32) * s
        return {'x': x, 'sg_w': sg_w, 'su_w': su_w, 'sd_w': sd_w, 'router_w': router_w, 'routing_bias': routing_bias, 'wg': wg, 'wu': wu, 'wd': wd}
    _L1_ffn_all = _L1_ffn_setup()
    _L1_ffn_in = {k: v for k, v in _L1_ffn_all.items() if k in ('sg_w', 'su_w', 'sd_w', 'router_w', 'routing_bias', 'wg', 'wu', 'wd')}
    del _L1_ffn_all
    return {'x': x, 'ctx_1024': ctx_1024, 'mask_BxSxS2_fk0': mask_BxSxS2_fk0, 'g_xattn': g_xattn, 'g_ffn': g_ffn, 'L0_xattn_Wq': _L0_xattn_in['Wq'], 'L0_xattn_bq': _L0_xattn_in['bq'], 'L0_xattn_Wk': _L0_xattn_in['Wk'], 'L0_xattn_bk': _L0_xattn_in['bk'], 'L0_xattn_Wv': _L0_xattn_in['Wv'], 'L0_xattn_bv': _L0_xattn_in['bv'], 'L0_ffn_w1': _L0_ffn_in['w1'], 'L0_ffn_b1': _L0_ffn_in['b1'], 'L0_ffn_w2': _L0_ffn_in['w2'], 'L0_ffn_b2': _L0_ffn_in['b2'], 'L1_xattn_Wq': _L1_xattn_in['Wq'], 'L1_xattn_bq': _L1_xattn_in['bq'], 'L1_xattn_Wk': _L1_xattn_in['Wk'], 'L1_xattn_bk': _L1_xattn_in['bk'], 'L1_xattn_Wv': _L1_xattn_in['Wv'], 'L1_xattn_bv': _L1_xattn_in['bv'], 'L1_ffn_sg_w': _L1_ffn_in['sg_w'], 'L1_ffn_su_w': _L1_ffn_in['su_w'], 'L1_ffn_sd_w': _L1_ffn_in['sd_w'], 'L1_ffn_router_w': _L1_ffn_in['router_w'], 'L1_ffn_routing_bias': _L1_ffn_in['routing_bias'], 'L1_ffn_wg': _L1_ffn_in['wg'], 'L1_ffn_wu': _L1_ffn_in['wu'], 'L1_ffn_wd': _L1_ffn_in['wd']}

def reference(x, ctx_1024, mask_BxSxS2_fk0, g_xattn, g_ffn, L0_xattn_Wq, L0_xattn_bq, L0_xattn_Wk, L0_xattn_bk, L0_xattn_Wv, L0_xattn_bv, L0_ffn_w1, L0_ffn_b1, L0_ffn_w2, L0_ffn_b2, L1_xattn_Wq, L1_xattn_bq, L1_xattn_Wk, L1_xattn_bk, L1_xattn_Wv, L1_xattn_bv, L1_ffn_sg_w, L1_ffn_su_w, L1_ffn_sd_w, L1_ffn_router_w, L1_ffn_routing_bias, L1_ffn_wg, L1_ffn_wu, L1_ffn_wd):
    import jax
    import jax.numpy as jnp

    def _L0_xattn_ref(Q, K, V, Wq, bq, Wk, bk, Wv, bv):
        import jax, jax.numpy as jnp
        import numpy as np
        H = 16
        DK = 64
        D_MODEL = 256
        B = Q.shape[0]

        def proj(x, W, b):
            y = jnp.einsum('btd,ed->bte', x, W) + b
            return y.reshape(B, -1, H, DK).transpose(0, 2, 1, 3)
        q = proj(Q, Wq, bq)
        k = proj(K, Wk, bk)
        v = proj(V, Wv, bv)
        scores = jnp.einsum('bhqd,bhkd->bhqk', q, k) / jnp.sqrt(jnp.float32(DK))
        attn = jax.nn.softmax(scores, axis=-1)
        out = jnp.einsum('bhqk,bhkd->bhqd', attn, v)
        return out.transpose(0, 2, 1, 3).reshape(B, -1, D_MODEL)

    def _L0_ffn_ref(x, w1, b1, w2, b2):
        import jax, jax.numpy as jnp
        import numpy as np
        EPS = 1e-08

        def _ste(x, q):
            return x + jax.lax.stop_gradient(q - x)

        def quant_act_uint8(x):
            s = jax.lax.stop_gradient(jnp.maximum(jnp.max(x), EPS)) / 255.0
            q = jnp.clip(jnp.round(x / s), 0.0, 255.0) * s
            return (_ste(x, q), s)

        def quant_weight_int8_perchannel(w):
            s = jax.lax.stop_gradient(jnp.maximum(jnp.max(jnp.abs(w), axis=1, keepdims=True), EPS)) / 127.0
            q = jnp.clip(jnp.round(w / s), -128.0, 127.0) * s
            return (_ste(w, q), s[:, 0])

        def quant_bias_int32(b, s_in, s_w):
            s = jax.lax.stop_gradient(s_in * s_w)
            q = jnp.round(b / s) * s
            return _ste(b, q)

        def quant_linear(x, w, b):
            xq, s_in = quant_act_uint8(x)
            wq, s_w = quant_weight_int8_perchannel(w)
            bq = quant_bias_int32(b, s_in, s_w)
            return jnp.einsum('btd,fd->btf', xq, wq) + bq
        h = jax.nn.relu(quant_linear(x, w1, b1))
        return quant_linear(h, w2, b2)

    def _L1_xattn_ref(primary, context_sequence, mask, Wq, bq, Wk, bk, Wv, bv):
        import jax, jax.numpy as jnp
        import numpy as np
        INPUT_DIM, ATTN_DIM, OUTPUT_DIM = (256, 256, 256)
        B, LQ, LKV = (4, 512, 512)
        q = primary @ Wq + bq
        k = context_sequence @ Wk + bk
        v = context_sequence @ Wv + bv
        score = jnp.einsum('bqd,bkd->bqk', q, k) / jnp.sqrt(jnp.float32(ATTN_DIM))
        score = score + mask * -1000000000.0
        attn = jax.nn.softmax(score, axis=-1)
        return jnp.einsum('bqk,bkd->bqd', attn, v)

    def _L1_ffn_ref(x, sg_w, su_w, sd_w, router_w, routing_bias, wg, wu, wd):
        import jax, jax.numpy as jnp
        import numpy as np
        H = 256
        I = 512
        E = 8
        TOP_K = 2
        NUM_SHARED = 1
        orig_shape = x.shape
        xt = x.reshape(-1, H)
        T = xt.shape[0]
        shared = jax.nn.silu(xt @ sg_w.T) * (xt @ su_w.T) @ sd_w.T
        shared = shared / NUM_SHARED
        logits = xt @ router_w.T + routing_bias
        probs = jax.nn.sigmoid(logits)
        topk_p, topk_idx = jax.lax.top_k(probs, TOP_K)
        topk_p = topk_p / jnp.sum(topk_p, axis=-1, keepdims=True)
        w = jnp.zeros((T, E), dtype=xt.dtype)
        w = w.at[jnp.arange(T)[:, None], topk_idx].add(topk_p)
        g = jnp.einsum('th,eih->tei', xt, wg)
        u = jnp.einsum('th,eih->tei', xt, wu)
        h = jax.nn.silu(g) * u
        y = jnp.einsum('tei,ehi->teh', h, wd)
        routed = jnp.einsum('te,teh->th', w, y)
        return (shared + routed).reshape(orig_shape)
    x = x + jnp.tanh(g_xattn[0]) * _L0_xattn_ref(_layernorm(x, axis=-1), ctx_1024, ctx_1024, L0_xattn_Wq, L0_xattn_bq, L0_xattn_Wk, L0_xattn_bk, L0_xattn_Wv, L0_xattn_bv)
    x = x + jnp.tanh(g_ffn[0]) * _L0_ffn_ref(_layernorm(x, axis=-1), L0_ffn_w1, L0_ffn_b1, L0_ffn_w2, L0_ffn_b2)
    x = x + jnp.tanh(g_xattn[1]) * _L1_xattn_ref(_layernorm(x, axis=-1), ctx_1024, mask_BxSxS2_fk0, L1_xattn_Wq, L1_xattn_bq, L1_xattn_Wk, L1_xattn_bk, L1_xattn_Wv, L1_xattn_bv)
    x = x + jnp.tanh(g_ffn[1]) * _L1_ffn_ref(_layernorm(x, axis=-1), L1_ffn_sg_w, L1_ffn_su_w, L1_ffn_sd_w, L1_ffn_router_w, L1_ffn_routing_bias, L1_ffn_wg, L1_ffn_wu, L1_ffn_wd)
    return x

_drawn_inputs = setup_inputs


def setup_inputs(seed=0):
    import zlib

    import numpy as np

    out = dict(_drawn_inputs(seed))
    spreads = {'g_ffn': (-1.0, 0.6), 'L1_ffn_routing_bias': (0.0, 0.8)}
    factors = {'L0_xattn_bq': 4.724,
     'L0_xattn_bk': 8.0,
     'L0_ffn_b1': 8.0,
     'L0_ffn_b2': 8.0,
     'L1_xattn_bq': 8.0,
     'L1_xattn_bk': 8.0,
     'L1_ffn_sg_w': 3.371,
     'L1_ffn_su_w': 3.222,
     'L1_ffn_sd_w': 3.226,
     'L1_ffn_router_w': 5.701,
     'L1_ffn_wg': 4.908,
     'L1_ffn_wu': 4.851,
     'L1_ffn_wd': 4.849}
    for name, (base, spread) in spreads.items():
        noise = np.random.default_rng([zlib.crc32(name.encode()), seed]).standard_normal(out[name].shape)
        drawn = base * np.exp(spread * noise) if base else spread * noise
        out[name] = jnp.asarray(drawn.astype(out[name].dtype))
    for name, factor in factors.items():
        out[name] = (out[name] * factor).astype(out[name].dtype)
    return out
```

```python
from contextlib import ExitStack

import numpy as np
import concourse.bass as bass
from concourse import mybir

F32 = mybir.dt.float32
F16 = mybir.dt.float16
BF16 = mybir.dt.bfloat16
I32 = mybir.dt.int32
ALU = mybir.AluOpType
ACT = mybir.ActivationFunctionType
AX = mybir.AxisListType
ds = bass.ds

P = 128
NB = 32
D = 256
KC = D // P
GB = 4
NG = NB // GB
GT = GB * P
NH0 = 4
BLK = 32
F = 1024
FC = F // P
E = 8
NE = E + 1
I = 512
IC = I // P
RT = 2 * NB + E
SLOTS = RT * P
EPS = 1e-5
QEPS = 1e-8
MAGIC = 12582912.0
XSCALE = 256.0

C_BQ0, C_BK0, C_BQ1, C_BK1, C_B1 = 0, 2, 4, 6, 8
NCOL = 16
R_BV0, R_BV1, R_B2, R_RB, R_GX, R_GF = 0, 256, 512, 768, 776, 778
NROW = 780
K_ID, K_TRI, K_ONE, K_I8, K_ROW, K_TILE = 0, 128, 256, 384, 392, 424
NCONST = 424 + RT
ROW = D + 2
NT = NB + RT
NO_ROW = 1.0e6


def at_least(n, k):
    return not isinstance(n, int) or n >= k


def run_tiles(eng, step):
    one = lambda n: step(n // 2, n % 2, None if n == NT else "shared" if n < NB else "slots", "shared" if n <= NB else "slots")
    for n in range(4):
        one(n)
    with eng.Fori(2, NB // 2) as i:
        step(i, 0, "shared", "shared")
        step(i, 1, "shared", "shared")
    for n in range(NB, NB + 4):
        one(n)
    with eng.Fori(NB // 2 + 2, NT // 2 - 1) as i:
        step(i, 0, "slots", "slots")
        step(i, 1, "slots", "slots")
    for n in range(NT - 2, NT + 1):
        one(n)


def counted(eng, value):
    if not isinstance(value, int):
        eng.compute_val(value)
    return value


class Chain:

    def __init__(self, eng, sem, base=0):
        self.eng, self.sem, self.base, self.n = eng, sem, base, 0

    def __call__(self, ins, held=None):
        self.n += 1
        ins.then_inc(self.sem, 1)
        count = counted(self.eng, self.base + self.n)
        if held is not None:
            self.eng.wait_ge(held, 1)
        self.eng.wait_ge(self.sem, count)


def bass_gated_two_layer(nc, x, ctxT, mask, wqkv0, wqkv1, cols, rows, w1, w2, wmoe, wrt, consts, out):
    ctx = ExitStack()
    with ctx:
        def sb(name, shape, dt=F32):
            return ctx.enter_context(nc.sbuf_tensor(name, shape, dt))

        def sem(name):
            return ctx.enter_context(nc.semaphore(name))

        X = sb("X", [P, NB, D])
        XNF = sb("XNF", [P, NB * ROW])
        XN = XNF[:, 0:NB * D].rearrange("p (b d) -> p b d", b=NB)
        XR = XNF[:, :].rearrange("p (b r) -> p b r", b=NB)
        WM_ELEMS = 3 * NE * 2 * 1024
        WM = sb("WM", [P, WM_ELEMS], F16)
        WMF = WM[:, :].bitcast(F32)
        used = [0]

        def arena(n, dt=F32):
            a = WMF[:, used[0]:used[0] + n]
            used[0] += n
            assert used[0] <= WM_ELEMS // 2
            return a if dt == F32 else a.bitcast(dt)

        cst = sb("cst", [P, NCONST])
        ident = cst[:, K_ID:K_ID + P]
        ones = cst[:, K_ONE:K_ONE + P]
        tri = cst[:, K_TRI:K_TRI + P]
        colv = sb("colv", [P, NCOL])
        rowv = sb("rowv", [P, NROW])
        small = sb("small", [P, 1100])
        so = [0]

        def sm(n):
            a = small[:, so[0]:so[0] + n]
            so[0] += n
            assert so[0] <= 1100
            return a

        tg = sm(4)
        neghalf = sm(4)
        bnst = [sm(6 * GB), sm(6 * GB)]
        mv = [sm(2 * GB), sm(2 * GB)]
        ve = [sm(GB), sm(GB)]
        rs1 = sm(GB)
        mu1 = sm(GB)
        nmr = sm(GB)
        rs2 = sm(NB)
        xmg = sm(GB)
        xmx = sm(NB)
        rmax = sm(16)
        rsum = sm(16)
        rinv = sm(16)
        t32 = sm(NB)
        g1 = sm(8)
        sc = sm(16)
        aq = sm(NB)
        cf = sm(FC)
        bf = sm(FC)
        ca = sm(FC)
        ba = sm(FC)
        hm = sm(FC)
        sw1 = sm(FC)
        iw1 = sm(FC)
        sw2 = sm(2)
        iw2 = sm(2)
        tf = sm(FC)

        wmx = sm(NE * 3)
        wm3 = sm(3)
        wa3 = sm(3)
        pw3 = sm(3)
        ip3 = sm(3)
        wsc = sm(3)
        cgs = sm(1)
        cus = sm(1)
        ysc = sm(1)
        negmax = sm(GB)
        mu4 = sm(NB)
        nm4 = sm(NB)
        w12 = [sm(NB), sm(NB)]
        mmax = [sm(NB), sm(NB)]
        imin = [sm(NB), sm(NB)]
        slotf = [sm(NB), sm(NB)]
        e8 = [sm(E) for _ in range(5)]
        oidx = [sm(1).bitcast(I32), sm(1).bitcast(I32)]

        WORK = 6144
        work = sb("work", [P, WORK])
        watt = work[:, 0:3 * KC * D].rearrange("p (w k d) -> p w k d", w=3, k=KC)
        wst = work[:, 1536:4608]
        PT = work[:, 4608:5120].rearrange("p (b q) -> p b q", b=GB)
        rt = [work[:, 256 * n:256 * (n + 1)] for n in range(8)]
        rt8 = work[:, 5848:5848 + ROW]
        xnb = work[:, 2048:3072].rearrange("p (b d) -> p b d", b=GB)
        xnbT = work[:, 3072:4096].rearrange("p (k t) -> p k t", k=KC)
        lg = rt[7]
        wrts = work[:, 5696:5696 + KC * E].rearrange("p (k e) -> p k e", k=KC)
        slot_i = [work[:, 5712 + NB * k:5712 + NB * (k + 1)].bitcast(I32) for k in range(2)]
        eidx = work[:, 5776:5776 + RT].bitcast(I32)
        mw = rt[0][:, 0:RT]
        mrow = rt[1][:, 0:RT].bitcast(I32)
        wo = [2048]

        def tw(n, dt=F32):
            w = work[:, wo[0]:wo[0] + n]
            wo[0] += n
            assert wo[0] <= 5696
            return w if dt == F32 else w.bitcast(dt)

        xt_ = [tw(ROW) for _ in range(2)]
        xh = [tw(KC * P // 2, F16).rearrange("p (k t) -> p k t", k=KC) for _ in range(2)]
        xl = [tw(KC * P // 2, F16).rearrange("p (k t) -> p k t", k=KC) for _ in range(2)]
        hs = [tw(I) for _ in range(2)]
        hh = [tw(I // 2, F16).rearrange("p (c t) -> p c t", c=IC) for _ in range(2)]
        hl = [tw(I // 2, F16).rearrange("p (c t) -> p c t", c=IC) for _ in range(2)]
        yb = [tw(D) for _ in range(2)]
        class Buffers:

            def __init__(s, words):
                s.ctxb = words(KC * GT).rearrange("p (k t) -> p k t", k=KC)
                s.xn = words(GB * D).rearrange("p (b d) -> p b d", b=GB)
                s.xnT = words(KC * GT).rearrange("p (k t) -> p k t", k=KC)
                s.qT = words(KC * GT).rearrange("p (k t) -> p k t", k=KC)
                s.kT = words(KC * GT).rearrange("p (k t) -> p k t", k=KC)
                s.v = words(GB * D).rearrange("p (b d) -> p b d", b=GB)
                s.S = words(512)
                s.otmp = words(GB * D).rearrange("p (b d) -> p b d", b=GB)

        B0 = Buffers(arena)
        ctxb, xn, xnT, qT, kT, v, otmp = B0.ctxb, B0.xn, B0.xnT, B0.qT, B0.kT, B0.v, B0.otmp
        S = B0.S.rearrange("p (s k) -> p s k", k=BLK)
        xw = [0]

        def xarena(n):
            a = XNF[:, xw[0]:xw[0] + n]
            xw[0] += n
            assert xw[0] <= NB * ROW
            return a

        B1 = Buffers(xarena)
        S1 = B1.S.rearrange("p (b k) -> p b k", b=GB)
        mk = xarena(GB * P).rearrange("p (b k) -> p b k", b=GB)
        BD = arena(16 * P).rearrange("p (s q) -> p s q", s=16)
        XQT = arena(NB * P * KC // 2, BF16).rearrange("p (k t) -> p k t", k=KC)
        hfm = arena(4 * GT)
        hf = [hfm[:, 2 * GT * n:2 * GT * (n + 1)].rearrange("p (a t) -> p a t", a=2) for n in range(2)]
        w1f = hfm.rearrange("p (f d) -> p f d", f=FC)
        hqm = [arena(FC * GT // 2) for _ in range(2)]
        hq = [z.bitcast(BF16).rearrange("p (f t) -> p f t", f=FC) for z in hqm]
        w2f = hqm[0].rearrange("p (c f) -> p c f", c=2)
        w1q = arena(FC * D // 2, BF16).rearrange("p (f d) -> p f d", f=FC)
        w2q = arena(2 * F // 2, BF16).rearrange("p (c f) -> p c f", c=2)
        w1T = arena(KC * F // 2, BF16).rearrange("p (k f) -> p k f", k=KC)
        w2T = arena(FC * D // 2, BF16).rearrange("p (f d) -> p f d", f=FC)
        identb = arena(P // 2, BF16)
        mxA = arena(NG * FC).rearrange("p (g f) -> p g f", g=NG)
        crow = arena(D)
        brow = arena(D)
        swrow = arena(D)
        trow = arena(D)
        xqf = arena(GB * D).rearrange("p (b d) -> p b d", b=GB)
        xqb = arena(GB * D // 2, BF16).rearrange("p (b d) -> p b d", b=GB)

        ps = ctx.enter_context(nc.psum_tensor("ps", [P, 8, 512], F32))
        psb = ps[:, :, :].bitcast(BF16)

        def pair(n):
            return ps[:, 2 * n:2 * n + 2, :]

        xs_dram = nc.dram_tensor("dispatched", (NT * P, ROW), F32).ap()
        sw_dram = nc.dram_tensor("sw2_scratch", (1, D), F32).ap()

        x_in = [sem(f"x_in{i}") for i in range(2)]
        c_in = sem("c_in")
        wat_in = sem("wat_in")
        ctx_in = sem("ctx_in")
        w12_in = sem("w12_in")
        rows_in = sem("rows_in")
        dchain = sem("dchain")
        mset = sem("mset")
        tg_ready = sem("tg_ready")

        class L:
            def __init__(s, n):
                s.ve1 = sem(f"a{n}_ve1")
                s.rstd1 = sem(f"a{n}_rstd1")
                s.nmr = sem(f"a{n}_nmr")
                s.xn = sem(f"a{n}_xn")
                s.xnT_ps = sem(f"a{n}_xnT_ps")
                s.xnT = sem(f"a{n}_xnT")
                s.q_ps = sem(f"a{n}_q_ps")
                s.q = sem(f"a{n}_q")
                s.k_ps = sem(f"a{n}_k_ps")
                s.k = sem(f"a{n}_k")
                s.v_ps = sem(f"a{n}_v_ps")
                s.v = sem(f"a{n}_v")
                s.s_ps = sem(f"a{n}_s_ps")
                s.s_sb = sem(f"a{n}_s_sb")
                s.sub = sem(f"a{n}_sub")
                s.exp = sem(f"a{n}_exp")
                s.pt_ps = sem(f"a{n}_pt_ps")
                s.pt = sem(f"a{n}_pt")
                s.pv_ps = sem(f"a{n}_pv_ps")
                s.pv = sem(f"a{n}_pv")
                s.res = sem(f"a{n}_res")
                s.ve2 = sem(f"a{n}_ve2")
                s.rstd2 = sem(f"a{n}_rstd2")
                s.d = sem(f"a{n}_d")
        A0 = L(0)
        A0.B = B0
        centred, xmx_done = sem("centred"), sem("xmx_done")
        gm_ready, gm_all = sem("gm_ready"), sem("gm_all")
        aq_ready = sem("aq_ready")
        xq_f, xq_b, xqT_ps, xqT_sb = sem("xq_f"), sem("xq_b"), sem("xqT_ps"), sem("xqT_sb")
        wq_ready, wT_ps, wT_sb = sem("wq_ready"), sem("wT_ps"), sem("wT_sb")
        sw2T_ps, sw2_sb, sw2_st, swrow_in = sem("sw2T_ps"), sem("sw2_sb"), sem("sw2_st"), sem("swrow_in")
        fa_ps, fa_max = sem("fa_ps"), sem("fa_max")
        hm_ready, hm_all, cb_ready = sem("hm_ready"), sem("hm_all"), sem("cb_ready")
        f1_ps, f1_act, f1_q = sem("f1_ps"), sem("f1_act"), sem("f1_q")
        f2_ps, f2_ev, f2_a, f2_res = sem("f2_ps"), sem("f2_ev"), sem("f2_a"), sem("f2_res")
        A1 = L(1)
        A1.B = B1
        ctx1_in, mask_in, mneg, nmx = sem("ctx1_in"), sem("mask_in"), sem("mneg"), sem("nmx")
        wst_in, wmax_done, wm_ready, wm_all, wsc_ready = sem("wst_in"), sem("wmax_done"), sem("wm_ready"), sem("wm_all"), sem("wsc_ready")
        whi, wlo = sem("whi"), sem("wlo")
        nm4_ready, xnb_ready, xr_copied, xnbT_ps, xnbT_sb, lg_ps, lg_sb = (sem("nm4_ready"), sem("xnb_ready"), sem("xr_copied"),
            sem("xnbT_ps"), sem("xnbT_sb"), sem("lg_ps"), sem("lg_sb"))
        wrt_in, xs_st, fill_ready, fill_st = sem("wrt_in"), sem("xs_st"), sem("fill_ready"), sem("fill_st")
        lgx, sig, oh_ready, rank_ps, slots_ready, w2_ready, sent = (sem("lgx"), sem("sig"), sem("oh_ready"), sem("rank_ps"),
            sem("slots_ready"), sem("w2_ready"), sem("sent"))
        oidx_ready = sem("oidx_ready")
        xt_in = [sem("xt_in0"), sem("xt_in1")]
        t_ps, t_hi, t_lo, g_ps, u_ps, silu, hid, h_ps, h_hi, h_lo, y_ps, y_sb, y_add, meta, out_st, y_out = (sem(n) for n in
            ("t_ps", "t_hi", "t_lo", "g_ps", "u_ps", "silu", "hid", "h_ps", "h_hi", "h_lo", "y_ps", "y_sb", "y_add", "meta", "out_st", "y_out"))

        block = ctx.enter_context(nc.Block())

        def xg(g):
            return X[:, ds(g * GB, GB), :] if not isinstance(g, int) else X[:, g * GB:(g + 1) * GB, :]

        def xt(t):
            return X[:, ds(t, 1), :].rearrange("p a d -> p (a d)") if not isinstance(t, int) else X[:, t, :]

        @block.sync
        def _(sp):
            sp.dma_start(X[:, 0:GB, :], x[:, 0:GB, :]).then_inc(x_in[0], 16)
            sp.dma_start(cst[:, :], consts).then_inc(c_in, 16)
            sp.dma_start(colv[:, :], cols).then_inc(c_in, 16)
            sp.dma_start(rowv[:, :], rows.partition_broadcast(P)).then_inc(c_in, 16)
            sp.dma_start(watt[:, :, :, :], wqkv0).then_inc(wat_in, 16)
            sp.dma_start(ctxb[:, :, :], ctxT[:, 0]).then_inc(ctx_in, 16)
            sp.dma_start(X[:, GB:NB, :], x[:, GB:NB, :]).then_inc(x_in[1], 16)
            sp.dma_start(w1f[:, :, :], w1).then_inc(w12_in, 16)
            sp.dma_start(w2f[:, :, :], w2).then_inc(w12_in, 16)
            sp.dma_start(wst, wmoe[:, 0].rearrange("p m w -> p (m w)")).then_inc(wst_in, 16)
            with sp.Fori(1, NG) as g:
                sp.wait_ge(A0.v_ps, g)
                sp.dma_start(ctxb[:, :, :], ctxT[:, ds(g, 1)].rearrange("p a k t -> p (a k) t")).then_inc(ctx_in, 16)
                sp.wait_ge(wmax_done, g)
                sp.dma_start(wst, wmoe[:, ds(g, 1)].rearrange("p a m w -> p (a m w)")).then_inc(wst_in, 16)
            sp.wait_ge(wmax_done, NG)
            sp.dma_start(wst, wmoe[:, NG].rearrange("p m w -> p (m w)")).then_inc(wst_in, 16)
            sp.wait_ge(A0.v_ps, NG)
            sp.dma_start(watt, wqkv1).then_inc(wat_in, 16)
            sp.wait_ge(sw2_sb, 1)
            sp.dma_start(sw_dram.rearrange("a (p c) -> p (a c)", p=P), sw2).then_inc(sw2_st, 16)
            sp.wait_ge(sw2_st, 16)
            sp.dma_start(swrow, sw_dram.partition_broadcast(P)).then_inc(swrow_in, 16)
            sp.wait_ge(wmax_done, NE)
            sp.dma_start(wst, wmoe[:, 0].rearrange("p m w -> p (m w)")).then_inc(wst_in, 16)
            sp.wait_ge(xq_f, NG)
            sp.dma_start(B1.ctxb, ctxT[:, 0]).then_inc(ctx1_in, 16)
            sp.dma_start(mk, mask[:, 0:GB, :]).then_inc(mask_in, 16)
            def attention1_loads(g, weights):
                sp.wait_ge(A1.v_ps, g)
                sp.dma_start(B1.ctxb, (ctxT[:, ds(g, 1)] if not isinstance(g, int) else ctxT[:, g:g + 1]).rearrange("p a k t -> p (a k) t")).then_inc(ctx1_in, 16)
                if weights:
                    sp.wait_ge(wlo, g - 1)
                    sp.dma_start(wst, wmoe[:, ds(g - 1, 1)].rearrange("p a m w -> p (a m w)")).then_inc(wst_in, 16)
                sp.wait_ge(A1.s_sb, g)
                sp.dma_start(mk, mask[:, ds(g * GB, GB), :] if not isinstance(g, int) else mask[:, g * GB:(g + 1) * GB, :]).then_inc(mask_in, 16)

            attention1_loads(1, False)
            with sp.Fori(2, NG) as g:
                attention1_loads(g, True)
            for e in (NG - 1, NG):
                sp.wait_ge(wlo, e)
                sp.dma_start(wst, wmoe[:, e].rearrange("p m w -> p (m w)")).then_inc(wst_in, 16)
            sp.wait_ge(wlo, NE)
            sp.dma_start(wrts, wrt).then_inc(wrt_in, 16)
            sp.wait_ge(fill_ready, 1)
            sp.dma_start(xs_dram[NB * P:NT * P, :].rearrange("(t p) r -> p t r", p=P),
                         rt8.rearrange("p (a r) -> p a r", a=1).to_broadcast([P, RT, ROW])).then_inc(fill_st, 16)
            with sp.Fori(0, NG) as g:
                sp.wait_ge(xr_copied, g + 1)
                sp.dma_start(xs_dram[ds(g * GT, GT), :].rearrange("(b p) r -> p b r", p=P)[:, :, 0:D],
                             XR[:, ds(g * GB, GB), 0:D]).then_inc(xs_st, 16)
            sp.wait_ge(xs_st, 16 * NG)
            sp.wait_ge(fill_st, 16)

            def load_tile(n, par, waits):
                if waits:
                    count = counted(sp, n - 1)
                    sp.wait_ge(x_in[0], 16)
                    sp.wait_ge(t_ps, count)
                    if waits == "slots":
                        sp.wait_ge(meta, n - (1 + NB))
                src = xs_dram[n * P:(n + 1) * P, :] if isinstance(n, int) else xs_dram[ds(n * P, P), :]
                w = D if (isinstance(n, int) and n < NB) or waits == "shared" else ROW
                sp.dma_start(xt_[par][:, 0:w], src[:, 0:w]).then_inc(xt_in[par], 16)

            sp.wait_ge(lg_sb, NG)
            load_tile(0, 0, None)
            load_tile(1, 1, None)
            load_tile(2, 0, "shared")
            load_tile(3, 1, "shared")
            with sp.Fori(2, NB // 2) as i:
                load_tile(i * 2, 0, "shared")
                load_tile(i * 2 + 1, 1, "shared")
                sp.wait_ge(y_add, i * 2 - 2)
                sp.dma_start(out[:, ds(i * 2 - 4, 2), :], X[:, ds(i * 2 - 4, 2), :]).then_inc(out_st, 16)
            sp.wait_ge(sent, 16 * 2 * NB)
            for k in range(2):
                sp.wait_ge(t_ps, NB - 1 + k)
                load_tile(NB + k, k, None)
            sp.wait_ge(y_add, NB)
            sp.dma_start(out[:, NB - 4:NB, :], X[:, NB - 4:NB, :]).then_inc(out_st, 16)
            with sp.Fori(NB // 2 + 1, NT // 2) as i:
                load_tile(i * 2, 0, "slots")
                load_tile(i * 2 + 1, 1, "slots")

        @block.gpsimd
        def _(pool):
            pool.wait_ge(mset, 1)

            def attention_pool(a, g, has_prev, has_next2, npv, stats):
                if has_prev:
                    count = counted(pool, npv * g)
                    pool.wait_ge(mset, 1)
                    pool.wait_ge(a.pv, count)
                    pool.tensor_tensor(xg(g - 1), xg(g - 1), a.otmp, ALU.add).then_inc(a.res, 1)
                if has_next2:
                    count = counted(pool, g + 3)
                    pool.wait_ge(mset, 1)
                    pool.wait_ge(a.ve1, count)
                    pool.wait_ge(a.xn, g + 2)
                    pool.tensor_tensor(rs1, ve[0], neghalf, ALU.pow).then_inc(a.rstd1, 1)
                if has_prev:
                    count = counted(pool, g)
                    pool.wait_ge(mset, 1)
                    pool.wait_ge(a.ve2, count)
                    pool.tensor_tensor(stats[:, ds(g * GB - GB, GB)] if not isinstance(g, int) else
                                       stats[:, (g - 1) * GB:g * GB], ve[1], neghalf, ALU.pow).then_inc(a.rstd2, 1)

            A0.otmp, A1.otmp = B0.otmp, B1.otmp
            a = A0
            for g in range(2):
                pool.wait_ge(a.ve1, g + 1)
                if g:
                    pool.wait_ge(a.xn, g)
                pool.tensor_tensor(rs1, ve[0], neghalf, ALU.pow).then_inc(a.rstd1, 1)
            attention_pool(a, 0, False, True, 2, rs2)
            with pool.Fori(1, NG - 2) as g:
                attention_pool(a, g, True, True, 2, rs2)
            attention_pool(a, NG - 2, True, False, 2, rs2)
            attention_pool(a, NG - 1, True, False, 2, rs2)
            attention_pool(a, NG, True, False, 2, rs2)

            pool.wait_ge(gm_ready, 1)
            pool.partition_all_reduce(g1[:, 1:2], g1[:, 0:1], P, bass.bass_isa.ReduceOp.max).then_inc(gm_all, 1)
            pool.wait_ge(hm_ready, 1)
            pool.partition_all_reduce(g1[:, 3:4], g1[:, 2:3], P, bass.bass_isa.ReduceOp.max).then_inc(hm_all, 1)
            pool.wait_ge(wm_ready, 1)
            pool.partition_all_reduce(wa3, wm3, P, bass.bass_isa.ReduceOp.max).then_inc(wm_all, 1)
            bb = brow.rearrange("p (a d) -> p a d", a=1).to_broadcast([P, GB, D])
            with pool.Fori(0, NG) as g:
                count = counted(pool, g + 1)
                pool.wait_ge(mset, 1)
                pool.wait_ge(f2_ev, count)
                pool.tensor_tensor(xg(g), xg(g), otmp, ALU.add).then_inc(f2_a, 1)
                count = counted(pool, g + 1)
                pool.wait_ge(mset, 1)
                pool.wait_ge(f2_a, count)
                pool.tensor_tensor(xg(g), xg(g), bb, ALU.add).then_inc(f2_res, 1)

            def negate_mask(g):
                count = counted(pool, 16 * g + 16)
                pool.wait_ge(mset, 1)
                pool.wait_ge(mask_in, count)
                pool.tensor_scalar(mk, mk, -1.0e9, None, ALU.mult).then_inc(mneg, 1)

            a = A1
            for g in range(2):
                pool.wait_ge(a.ve1, g + 1)
                if g:
                    pool.wait_ge(a.xn, g)
                pool.tensor_tensor(rs1, ve[0], neghalf, ALU.pow).then_inc(a.rstd1, 1)
            negate_mask(0)
            attention_pool(a, 0, False, True, 1, rs2)
            with pool.Fori(1, NG - 2) as g:
                negate_mask(g)
                attention_pool(a, g, True, True, 1, rs2)
            for g in (NG - 2, NG - 1):
                negate_mask(g)
                attention_pool(a, g, True, False, 1, rs2)
            attention_pool(a, NG, True, False, 1, rs2)

            pool.wait_ge(slots_ready, 1)
            pool.wait_ge(fill_st, 16)
            pool.wait_ge(xs_st, 16 * NG)
            for k in range(2):
                if k:
                    pool.wait_ge(sent, 16 * NB)
                    pool.tensor_copy(XR[:, :, D], w12[1]).then_inc(w2_ready, 1)
                    pool.wait_ge(w2_ready, 1)
                for t in range(NB):
                    pool.indirect_dma_start(out=xs_dram, out_offset=bass.IndirectOffsetOnAxis(ap=slot_i[k][:, t:t + 1].bitcast(mybir.dt.uint32), axis=0),
                                            in_=XR[:, t, :], in_offset=None, bounds_check=NT * P - 1, oob_is_err=False).then_inc(sent, 16)
            out_rows = out.rearrange("p b d -> (p b) d")
            pool.wait_ge(out_st, 16 * (NB // 2 - 1))

            def add_rows(r, par, first):
                count = counted(pool, r + 1)
                pool.wait_ge(mset, 1)
                pool.wait_ge(meta, count)
                src = mrow[:, r:r + 1] if isinstance(r, int) else mrow[:, ds(r, 1)]
                pool.tensor_copy(oidx[par], src).then_inc(oidx_ready, 1)
                pool.wait_ge(oidx_ready, r + 1)
                pool.wait_ge(y_sb, r + 1)
                if not first:
                    count = counted(pool, r * 16)
                    pool.wait_ge(mset, 1)
                    pool.wait_ge(y_out, count)
                pool.indirect_dma_start(out=out_rows, out_offset=bass.IndirectOffsetOnAxis(ap=oidx[par].bitcast(mybir.dt.uint32), axis=0),
                                        in_=yb[par], in_offset=None, bounds_check=NB * P - 1, oob_is_err=False,
                                        compute_op=ALU.add).then_inc(y_out, 16)

            add_rows(0, 0, True)
            add_rows(1, 1, False)
            with pool.Fori(1, RT // 2) as i:
                add_rows(i * 2, 0, False)
                add_rows(i * 2 + 1, 1, False)
            pool.wait_ge(y_out, 16 * RT)

        @block.scalar
        def _(act):
            act.wait_ge(c_in, 48)
            act.activation(tg, rowv[:, R_GX:R_GX + 4], ACT.Tanh).then_inc(tg_ready, 1)

            def normalise(a, g):
                act.wait_ge(a.nmr, g + 1)
                if not (isinstance(g, int) and g == 0):
                    act.wait_ge(a.xnT_ps, g)
                for b in range(GB):
                    src = xt(g * GB + b)
                    last = act.activation(a.B.xn[:, b, :], src, ACT.Identity, bias=nmr[:, b:b + 1], scale=rs1[:, b:b + 1])
                last.then_inc(a.xn, 1)

            def evac_xnT(a, g, pr):
                act.wait_ge(a.xnT_ps, g + 1)
                act.activation(a.B.xnT, pair(pr), ACT.Copy).then_inc(a.xnT, 1)

            def evac_proj(ps_sem, sb_sem, dst, pr, col, g, free_sem):
                act.wait_ge(ps_sem, g + 1)
                if free_sem is not None:
                    act.wait_ge(free_sem[0], free_sem[1])
                for c in range(KC):
                    last = act.activation(dst[:, c, :], pair(pr)[:, c, :], ACT.Identity, bias=colv[:, col + c:col + c + 1])
                last.then_inc(sb_sem, 1)

            def attention0_act(a, g, has_prev, has_next):
                free = (a.s_ps, 2 * g) if has_prev else None
                evac_proj(a.q_ps, a.q, qT, 0, C_BQ0, g, free)
                if has_next:
                    normalise(a, g + 1)
                evac_proj(a.k_ps, a.k, kT, 1, C_BK0, g, None)
                if has_next:
                    evac_xnT(a, g + 1, 1)
                if has_prev:
                    act.wait_ge(a.pt, g)
                for h in range(2):
                    act.wait_ge(a.s_ps, 2 * g + h + 1)
                    for c in range(4):
                        r = slice(BLK * c, BLK * (c + 1))
                        dst = S[r, 8 * h:8 * h + 8, :].rearrange("p (m a) k -> p a m k", a=2)
                        src = pair(2 + h)[r, :, :].rearrange("p a (m q) -> p a m q", m=4)[:, :, :, r]
                        for par in range(2):
                            last = act.activation(dst[:, par], src[:, par], ACT.Copy)
                    last.then_inc(a.s_sb, 1)
                act.wait_ge(a.sub, g + 1)
                act.activation(S[:, :, :], S[:, :, :], ACT.Exp, scale=0.125).then_inc(a.exp, 1)

            a = A0
            normalise(a, 0)
            evac_xnT(a, 0, 1)
            attention0_act(a, 0, False, True)
            with act.Fori(1, NG - 1) as g:
                attention0_act(a, g, True, True)
            attention0_act(a, NG - 1, True, False)

            act.wait_ge(aq_ready, 1)
            with act.Fori(0, NG) as g:
                for b in range(GB):
                    last = act.activation(xqf[:, b, :], XN[:, ds(g * GB + b, 1), :].rearrange("p a d -> p (a d)"),
                                          ACT.Identity, bias=sc[:, 8:9], scale=aq[:, ds(g * GB + b, 1)])
                last.then_inc(xq_f, 1)
                act.wait_ge(xqT_ps, g + 1)
                act.activation(XQT[:, :, ds(g * GT, GT)], psb[:, 7, :].rearrange("p (k t) -> p k t", k=KC), ACT.Copy).then_inc(xqT_sb, 1)
            act.wait_ge(cb_ready, 1)
            with act.Fori(0, NG // 2) as i:
                for n in range(8):
                    act.wait_ge(f1_ps, i * 8 + n + 1)
                    if n >= 2:
                        act.wait_ge(f1_q, i * 8 + n - 1)
                    for k in range(2):
                        f = 2 * (n % 4) + k
                        last = act.activation(hf[n % 2][:, k, :], pair(n % 3)[:, k, :], ACT.Relu,
                                              bias=ba[:, f:f + 1], scale=ca[:, f:f + 1])
                    last.then_inc(f1_act, 1)

            def split_hi(e, parts=(0, 1, 2)):
                act.wait_ge(wst_in, (NE + 1) * 16 + e * 16)
                for m in parts:
                    off = e * 6144 + m * 2048
                    dst = WM[:, ds(off, 1024)] if not isinstance(e, int) else WM[:, off:off + 1024]
                    act.activation(dst, wst[:, m * 1024:(m + 1) * 1024], ACT.Identity, scale=wsc[:, m:m + 1]).then_inc(whi, 1)

            def attention1_act(a, g, has_prev, has_next):
                free = (a.s_ps, g) if has_prev else None
                evac_proj(a.q_ps, a.q, B1.qT, 0, C_BQ1, g, free)
                if has_prev:
                    split_hi(g - 1, (0, 1))
                if has_next:
                    normalise(a, g + 1)
                evac_proj(a.k_ps, a.k, B1.kT, 1, C_BK1, g, None)
                if has_prev:
                    split_hi(g - 1, (2,))
                    act.wait_ge(a.pt_ps, g)
                    act.activation(PT, ps[:, 4, :].rearrange("p (b q) -> p b q", b=GB), ACT.Copy).then_inc(a.pt, 1)
                if has_next:
                    evac_xnT(a, g + 1, 1)
                act.wait_ge(nmx, g + 1)
                if has_prev:
                    act.wait_ge(a.sub, g)
                for b in range(GB):
                    last = act.activation(S1[:, b, :], S1[:, b, :], ACT.Exp, bias=negmax[:, b:b + 1], accum_out=rsum[:, b:b + 1])
                last.then_inc(a.exp, 1)

            a = A1
            act.wait_ge(wsc_ready, 1)
            normalise(a, 0)
            evac_xnT(a, 0, 1)
            attention1_act(a, 0, False, True)
            with act.Fori(1, NG - 1) as g:
                attention1_act(a, g, True, True)
            attention1_act(a, NG - 1, True, False)
            act.wait_ge(a.pt_ps, NG)
            act.activation(PT, ps[:, 4, :].rearrange("p (b q) -> p b q", b=GB), ACT.Copy).then_inc(a.pt, 1)
            split_hi(NG - 1)
            split_hi(NG)

            act.wait_ge(nm4_ready, 1)
            with act.Fori(0, NG) as g:
                for b in range(GB):
                    t = g * GB + b
                    last = act.activation(xnb[:, b, :], xt(t), ACT.Identity, bias=nm4[:, ds(t, 1)], scale=rs2[:, ds(t, 1)])
                last.then_inc(xnb_ready, 1)
                act.wait_ge(xnbT_ps, g + 1)
                act.activation(xnbT, pair(0), ACT.Copy).then_inc(xnbT_sb, 1)
                act.wait_ge(xr_copied, g + 1)
            act.wait_ge(lgx, 1)
            act.activation(lg, lg, ACT.Exp, scale=-1.0).then_inc(sig, 1)

            def x_hi(n, par):
                act.wait_ge(t_ps, n + 1)
                if at_least(n, 2):
                    act.wait_ge(u_ps, n - 1)
                act.activation(xh[par], ps[:, 5, 0:D].rearrange("p (k t) -> p k t", k=KC), ACT.Copy, scale=XSCALE).then_inc(t_hi, 1)

            def tile_act(i, par, phase, prev_phase):
                n = i * 2 + par
                if at_least(n, 1):
                    act.wait_ge(h_ps, n)
                    if at_least(n, 3):
                        act.wait_ge(y_ps, n - 2)
                    act.activation(hh[1 - par], ps[:, 4, :].rearrange("p (c t) -> p c t", c=IC), ACT.Copy).then_inc(h_hi, 1)
                if phase:
                    act.wait_ge(g_ps, n + 1)
                    if at_least(n, 2):
                        act.wait_ge(h_ps, n - 1)
                    act.activation(hs[par], ps[:, 2 * par, :], ACT.Silu, scale=cgs[:, 0:1]).then_inc(silu, 1)
                if not (isinstance(n, int) and n + 1 >= NT):
                    x_hi(n + 1, 1 - par)
                if prev_phase == "slots":
                    r = n - (1 + NB)
                    act.wait_ge(y_ps, n)
                    act.wait_ge(meta, r + 1)
                    if at_least(r, 2):
                        act.wait_ge(y_out, r * 16 - 16)
                    w = mw[:, r:r + 1] if isinstance(r, int) else mw[:, ds(r, 1)]
                    act.activation(yb[1 - par], ps[:, 7 - par, 0:D], ACT.Identity, scale=w).then_inc(y_sb, 1)

            x_hi(0, 0)
            run_tiles(act, tile_act)

        @block.vector
        def _(dve):
            link = Chain(dve, dchain)
            dve.memset(neghalf, -0.5).then_inc(mset, 1)
            dve.memset(sc[:, 8:9], MAGIC)
            link(dve.memset(BD, 0.0))

            def stats1(a, g, ch, between=None):
                if not (isinstance(g, int) and g == 0):
                    dve.wait_ge(a.xn, g)
                for b in range(GB):
                    last = dve.bn_stats(bnst[0][:, 6 * b:6 * b + 6], xt(g * GB + b))
                ch(last, mset)
                for b in range(GB):
                    last = dve.bn_aggr(mv[0][:, 2 * b:2 * b + 2], bnst[0][:, 6 * b:6 * b + 6])
                ch(last)
                dve.tensor_scalar(ve[0], mv[0].rearrange("p (b t) -> p t b", t=2)[:, 1, :], EPS, None, ALU.add).then_inc(a.ve1, 1)
                if between:
                    between()
                dve.wait_ge(a.rstd1, g + 1)
                dve.scalar_tensor_tensor(out=nmr, in0=mv[0].rearrange("p (b t) -> p t b", t=2)[:, 0, :], scalar=-1.0,
                                         in1=rs1, op0=ALU.mult, op1=ALU.mult).then_inc(a.nmr, 1)

            bv0 = rowv[:, R_BV0:R_BV0 + D].rearrange("p (a d) -> p a d", a=1).to_broadcast([P, GB, D])

            def evac_pv0(a, g):
                for h in range(2):
                    dve.wait_ge(a.pv_ps, 2 * g + h + 1)
                    if h == 0 and not (isinstance(g, int) and g == 0):
                        dve.wait_ge(a.res, g)
                    dve.tensor_tensor(otmp[:, 2 * h:2 * h + 2, :].rearrange("p b (j k) -> p (b j) k", k=64),
                                      pair(2 + h)[:, 0, :].rearrange("p (s k) -> p s k", k=64),
                                      rinv[:, 8 * h:8 * h + 8].rearrange("p (s a) -> p s a", a=1).to_broadcast([P, 8, 64]),
                                      ALU.mult).then_inc(a.pv, 1)

            def after0(a, g, ch):
                dve.wait_ge(a.res, g + 1)
                for b in range(GB):
                    last = dve.bn_stats(bnst[1][:, 6 * b:6 * b + 6], xt(g * GB + b))
                ch(last, mset)
                for b in range(GB):
                    last = dve.bn_aggr(mv[1][:, 2 * b:2 * b + 2], bnst[1][:, 6 * b:6 * b + 6])
                ch(last)
                if not (isinstance(g, int) and g == 0):
                    dve.wait_ge(a.rstd2, g)
                dve.tensor_scalar(ve[1], mv[1].rearrange("p (b t) -> p t b", t=2)[:, 1, :], EPS, None, ALU.add).then_inc(a.ve2, 1)

            def centre0(a, g):
                for b in range(GB):
                    last = dve.tensor_scalar(XN[:, ds(g * GB + b, 1), :].rearrange("p a d -> p (a d)") if not isinstance(g, int) else XN[:, g * GB + b, :],
                                             xt(g * GB + b), mv[1][:, 2 * b:2 * b + 1], None, ALU.subtract)
                last.then_inc(centred, 1)

            def max0(g):
                dve.wait_ge(centred, g + 1)
                gs = XN[:, ds(g * GB, GB), :] if not isinstance(g, int) else XN[:, g * GB:(g + 1) * GB, :]
                dve.tensor_reduce(xmx[:, ds(g * GB, GB)] if not isinstance(g, int) else xmx[:, g * GB:(g + 1) * GB],
                                  gs, AX.X, ALU.max).then_inc(xmx_done, 1)

            def weight_max(e):
                dve.wait_ge(wst_in, 16 * e + 16)
                o = wmx[:, 3 * e:3 * e + 3] if isinstance(e, int) else wmx[:, ds(e * 3, 3)]
                dve.tensor_reduce(o, wst.rearrange("p (m w) -> p m w", m=3), AX.X, ALU.max, apply_absolute_value=True).then_inc(wmax_done, 1)

            def attention0_dve(a, g, ch, has_prev, has_next2):
                if has_prev:
                    evac_pv0(a, g - 1)
                dve.wait_ge(a.v_ps, g + 1)
                dve.tensor_tensor(v[:, :, :], pair(0).rearrange("p a (b d) -> p (a b) d", d=D), bv0, ALU.add).then_inc(a.v, 1)
                after = (lambda: after0(a, g - 1, ch)) if has_prev else None
                if has_next2:
                    stats1(a, g + 2, ch, after)
                elif after:
                    after()
                dve.wait_ge(a.s_sb, 2 * g + 2)
                ch(dve.tensor_reduce(rmax, S[:, :, :], AX.X, ALU.max))
                dve.tensor_tensor(S[:, :, :], S[:, :, :], rmax.rearrange("p (s a) -> p s a", a=1).to_broadcast([P, 16, BLK]),
                                  ALU.subtract).then_inc(a.sub, 1)
                if has_prev:
                    centre0(a, g - 1)
                dve.wait_ge(a.exp, g + 1)
                ch(dve.tensor_reduce(rsum, S[:, :, :], AX.X, ALU.add))
                ch(dve.reciprocal(rinv, rsum))
                dve.tensor_scalar(rinv, rinv, tg[:, 0:1], None, ALU.mult)
                for c in range(4):
                    r = slice(BLK * c, BLK * (c + 1))
                    last = dve.transpose(BD[r, :, r], S[r, :, :])
                last.then_inc(a.pt, 1)
                if has_prev:
                    max0(g - 1)
                weight_max(g)

            def quantise_weights():
                dve.wait_ge(w12_in, 32)
                link(dve.tensor_reduce(sw1, w1f, AX.X, ALU.max, apply_absolute_value=True))
                link(dve.tensor_reduce(sw2, w2f, AX.X, ALU.max, apply_absolute_value=True))
                link(dve.tensor_scalar(sw1, sw1, QEPS, 1.0 / 127.0, ALU.max, ALU.mult))
                ins = dve.tensor_scalar(sw2, sw2, QEPS, 1.0 / 127.0, ALU.max, ALU.mult)
                ins.then_inc(sw2_sb, 1)
                dve.wait_ge(sw2_sb, 1)
                link(dve.reciprocal(iw1, sw1))
                link(dve.reciprocal(iw2, sw2))
                for f in range(FC):
                    last = dve.tensor_scalar(w1f[:, f, :], w1f[:, f, :], iw1[:, f:f + 1], MAGIC, ALU.mult, ALU.add)
                for c in range(2):
                    last = dve.tensor_scalar(w2f[:, c, :], w2f[:, c, :], iw2[:, c:c + 1], MAGIC, ALU.mult, ALU.add)
                link(last)
                dve.tensor_scalar(w1q, w1f, MAGIC, None, ALU.subtract)
                dve.tensor_scalar(w2q, w2f, MAGIC, None, ALU.subtract).then_inc(wq_ready, 1)

            a = A0
            CH0 = 7
            dve.wait_ge(x_in[0], 16)
            stats1(a, 0, link)
            dve.wait_ge(x_in[1], 16)
            stats1(a, 1, link)
            dve.wait_ge(c_in, 48)
            dve.wait_ge(tg_ready, 1)
            dve.tensor_copy(identb, ident)
            quantise_weights()
            attention0_dve(a, 0, link, False, True)
            with dve.Fori(1, NG - 2) as g:
                ch = Chain(dve, a.d, (g - 1) * CH0)
                attention0_dve(a, g, ch, True, True)
                assert ch.n == CH0, ch.n
            for g in (NG - 2, NG - 1):
                attention0_dve(a, g, link, True, False)
            evac_pv0(a, NG - 1)
            after0(a, NG - 1, link)
            centre0(a, NG - 1)
            max0(NG - 1)

            weight_max(E)
            dve.wait_ge(wmax_done, NE)
            dve.tensor_reduce(wm3, wmx.rearrange("p (e m) -> p m e", m=3), AX.X, ALU.max).then_inc(wm_ready, 1)

            dve.wait_ge(a.rstd2, NG)
            dve.wait_ge(xmx_done, NG)
            link(dve.tensor_tensor(t32, xmx, rs2, ALU.mult))
            dve.tensor_reduce(g1[:, 0:1], t32, AX.X, ALU.max).then_inc(gm_ready, 1)
            dve.wait_ge(gm_all, 1)
            link(dve.tensor_scalar(sc[:, 0:1], g1[:, 1:2], QEPS, 1.0 / 255.0, ALU.max, ALU.mult))
            link(dve.reciprocal(sc[:, 1:2], sc[:, 0:1]))
            dve.tensor_scalar(aq, rs2, sc[:, 1:2], None, ALU.mult).then_inc(aq_ready, 1)
            link(dve.tensor_scalar(cf, sw1, sc[:, 0:1], None, ALU.mult))
            link(dve.reciprocal(tf, cf))
            link(dve.tensor_tensor(tf, tf, colv[:, C_B1:C_B1 + FC], ALU.mult))
            link(dve.tensor_scalar(tf, tf, MAGIC, MAGIC, ALU.add, ALU.subtract))
            link(dve.tensor_tensor(bf, tf, cf, ALU.mult))
            for w in range(2):
                dve.wait_ge(wT_ps, w + 1)
                dst, src = (w1T, psb[:, 0:2, :]) if w == 0 else (w2T, psb[:, 2:4, :])
                if w == 0:
                    dve.tensor_copy(dst, src).then_inc(wT_sb, 1)
                else:
                    dve.tensor_copy(dst.rearrange("p (a f) d -> p a (f d)", a=2), src).then_inc(wT_sb, 1)

            def round_rows(g):
                dve.wait_ge(xq_f, g + 1)
                if not (isinstance(g, int) and g == 0):
                    dve.wait_ge(xqT_ps, g)
                dve.tensor_scalar(xqb, xqf, -MAGIC, 0.0, ALU.add, ALU.max).then_inc(xq_b, 1)

            def hidden_max(i, last_pair):
                for half in range(2):
                    if not (last_pair and half):
                        round_rows(i * 2 + half + 1)
                    for q in range(4):
                        n = 4 * half + q
                        dve.wait_ge(fa_ps, i * 8 + n + 1)
                        gg = i * 2 + half
                        o = mxA[:, ds(gg, 1), 2 * q:2 * q + 2] if not isinstance(gg, int) else mxA[:, gg:gg + 1, 2 * q:2 * q + 2]
                        dve.tensor_reduce(o.rearrange("p a f -> p (a f)"), pair(n % 3), AX.X, ALU.max).then_inc(fa_max, 1)

            round_rows(0)
            with dve.Fori(0, NG // 2 - 1) as i:
                hidden_max(i, False)
            hidden_max(NG // 2 - 1, True)
            dve.wait_ge(fa_max, 4 * NG)
            link(dve.tensor_reduce(hm, mxA.rearrange("p g f -> p f g"), AX.X, ALU.max))
            link(dve.tensor_tensor(hm, hm, cf, ALU.mult))
            link(dve.tensor_tensor(hm, hm, bf, ALU.add))
            dve.tensor_reduce(g1[:, 2:3], hm, AX.X, ALU.max).then_inc(hm_ready, 1)
            dve.wait_ge(hm_all, 1)
            link(dve.tensor_scalar(sc[:, 2:3], g1[:, 3:4], QEPS, 1.0 / 255.0, ALU.max, ALU.mult))
            link(dve.reciprocal(sc[:, 3:4], sc[:, 2:3]))
            dve.tensor_scalar(ca, cf, sc[:, 3:4], None, ALU.mult)
            dve.tensor_scalar(ba, bf, sc[:, 3:4], None, ALU.mult).then_inc(cb_ready, 1)
            dve.wait_ge(swrow_in, 16)
            link(dve.tensor_scalar(trow.rearrange("p (c q) -> p c q", c=2), swrow.rearrange("p (q c) -> p c q", c=2),
                                   sc[:, 2:3], None, ALU.mult))
            link(dve.reciprocal(brow, trow))
            link(dve.tensor_tensor(brow, brow, rowv[:, R_B2:R_B2 + D], ALU.mult))
            link(dve.tensor_scalar(brow, brow, MAGIC, MAGIC, ALU.add, ALU.subtract))
            link(dve.scalar_tensor_tensor(out=brow, in0=brow, scalar=tg[:, 2:3], in1=trow, op0=ALU.mult, op1=ALU.mult))
            link(dve.tensor_scalar(crow, trow, tg[:, 2:3], None, ALU.mult))
            cb = crow.rearrange("p (a d) -> p a d", a=1).to_broadcast([P, GB, D])

            def hidden_round(i):
                for n in range(8):
                    dve.wait_ge(f1_act, i * 8 + n + 1)
                    q = n % 4
                    dve.tensor_scalar(hq[n // 4][:, 2 * q:2 * q + 2, :], hf[n % 2], MAGIC, MAGIC, ALU.add, ALU.subtract).then_inc(f1_q, 1)
                for half in range(2):
                    gg = i * 2 + half
                    dve.wait_ge(f2_ps, gg + 1)
                    if not (isinstance(gg, int) and gg == 0):
                        dve.wait_ge(f2_a, gg)
                    dve.tensor_tensor(otmp, pair(3 - half).rearrange("p a (b d) -> p (a b) d", d=D), cb, ALU.mult).then_inc(f2_ev, 1)

            hidden_round(0)
            with dve.Fori(1, NG // 2) as i:
                hidden_round(i)

            dve.wait_ge(wm_all, 1)
            link(dve.tensor_scalar(wa3, wa3, 2.0 ** -30, None, ALU.max))
            link(dve.tensor_scalar(pw3.bitcast(I32), wa3.bitcast(I32), 0x7F800000, None, ALU.bitwise_and))
            link(dve.reciprocal(ip3, pw3))
            dve.tensor_scalar(cgs, pw3[:, 0:1], 2.0 ** -21, None, ALU.mult)
            dve.tensor_scalar(cus, ip3[:, 0:1], 2.0 ** -24, None, ALU.mult)
            link(dve.tensor_tensor(ysc, pw3[:, 0:1], pw3[:, 1:2], ALU.mult))
            link(dve.tensor_tensor(ysc, ysc, pw3[:, 2:3], ALU.mult))
            link(dve.tensor_scalar(ysc, ysc, 2.0 ** -10, tg[:, 3:4], ALU.mult, ALU.mult))
            dve.tensor_scalar(wsc, ip3, 2.0 ** 13, None, ALU.mult).then_inc(wsc_ready, 1)

            bv1 = rowv[:, R_BV1:R_BV1 + D].rearrange("p (a d) -> p a d", a=1).to_broadcast([P, GB, D])

            def split_lo(e):
                for m in range(3):
                    dve.wait_ge(whi, e * 3 + m + 1)
                    off = e * 6144 + m * 2048
                    hi = WM[:, ds(off, 1024)] if not isinstance(e, int) else WM[:, off:off + 1024]
                    lo = WM[:, ds(off + 1024, 1024)] if not isinstance(e, int) else WM[:, off + 1024:off + 2048]
                    last = dve.scalar_tensor_tensor(out=lo, in0=wst[:, m * 1024:(m + 1) * 1024], scalar=wsc[:, m:m + 1],
                                                    in1=hi, op0=ALU.mult, op1=ALU.subtract)
                last.then_inc(wlo, 1)

            def evac_pv1(a, g):
                dve.wait_ge(a.pv_ps, g + 1)
                dve.wait_ge(a.sub, g + 1)
                if at_least(g, 1):
                    dve.wait_ge(a.res, g)
                dve.tensor_tensor(B1.otmp, pair(3).rearrange("p a (b d) -> p (a b) d", d=D),
                                  rinv[:, 0:GB].rearrange("p (s a) -> p s a", a=1).to_broadcast([P, GB, D]), ALU.mult).then_inc(a.pv, 1)

            def after1(a, g, ch):
                dve.wait_ge(a.res, g + 1)
                for b in range(GB):
                    last = dve.bn_stats(bnst[1][:, 6 * b:6 * b + 6], xt(g * GB + b))
                ch(last, mset)
                for b in range(GB):
                    last = dve.bn_aggr(mv[1][:, 2 * b:2 * b + 2], bnst[1][:, 6 * b:6 * b + 6])
                ch(last)
                if at_least(g, 1):
                    dve.wait_ge(a.rstd2, g)
                mvt = mv[1].rearrange("p (b t) -> p t b", t=2)
                dve.tensor_scalar(ve[1], mvt[:, 1, :], EPS, None, ALU.add).then_inc(a.ve2, 1)
                o = mu4[:, ds(g * GB, GB)] if not isinstance(g, int) else mu4[:, g * GB:(g + 1) * GB]
                ch(dve.tensor_copy(o, mvt[:, 0, :]))

            def attention1_dve(a, g, ch, has_prev, has_next2):
                if has_prev:
                    split_lo(g - 1)
                    evac_pv1(a, g - 1)
                dve.wait_ge(a.v_ps, g + 1)
                dve.tensor_tensor(B1.v, pair(0).rearrange("p a (b d) -> p (a b) d", d=D), bv1, ALU.add).then_inc(a.v, 1)
                dve.wait_ge(a.s_ps, g + 1)
                dve.wait_ge(mneg, g + 1)
                if has_prev:
                    dve.wait_ge(a.pt_ps, g)
                dve.scalar_tensor_tensor(out=S1, in0=ps[:, 5, :].rearrange("p (b k) -> p b k", b=GB), scalar=1.0 / 16.0,
                                         in1=mk, op0=ALU.mult, op1=ALU.add).then_inc(a.s_sb, 1)
                dve.wait_ge(a.s_sb, g + 1)
                ch(dve.tensor_reduce(rmax[:, 0:GB], S1, AX.X, ALU.max))
                dve.tensor_scalar(negmax, rmax[:, 0:GB], -1.0, None, ALU.mult).then_inc(nmx, 1)
                after = (lambda: after1(a, g - 1, ch)) if has_prev else None
                if has_next2:
                    dve.wait_ge(f2_res, g + 3)
                    stats1(a, g + 2, ch, after)
                elif after:
                    after()
                dve.wait_ge(a.exp, g + 1)
                ch(dve.reciprocal(rinv[:, 0:GB], rsum[:, 0:GB]))
                dve.tensor_scalar(rinv[:, 0:GB], rinv[:, 0:GB], tg[:, 1:2], None, ALU.mult).then_inc(a.sub, 1)

            a = A1
            CH1 = 7
            dve.wait_ge(f2_res, 2)
            stats1(a, 0, link)
            stats1(a, 1, link)
            attention1_dve(a, 0, link, False, True)
            with dve.Fori(1, NG - 2) as g:
                ch = Chain(dve, a.d, (g - 1) * CH1)
                attention1_dve(a, g, ch, True, True)
                assert ch.n == CH1, ch.n
            for g in (NG - 2, NG - 1):
                attention1_dve(a, g, link, True, False)
            evac_pv1(a, NG - 1)
            after1(a, NG - 1, link)
            split_lo(NG - 1)
            split_lo(E)
            dve.wait_ge(a.rstd2, NG)
            dve.scalar_tensor_tensor(out=nm4, in0=mu4, scalar=-1.0, in1=rs2, op0=ALU.mult, op1=ALU.mult).then_inc(nm4_ready, 1)

            link(dve.memset(rt8, 0.0))
            dve.memset(rt8[:, D + 1:D + 2], NO_ROW).then_inc(fill_ready, 1)

            rb = rowv[:, R_RB:R_RB + E].rearrange("p (a e) -> p a e", a=1).to_broadcast([P, GB, E])
            with dve.Fori(0, NG) as g:
                dve.wait_ge(xnb_ready, g + 1)
                dve.tensor_copy(XR[:, ds(g * GB, GB), 0:D], xnb).then_inc(xr_copied, 1)
                dve.wait_ge(lg_ps, g + 1)
                dve.tensor_tensor(lg[:, ds(g * GB * E, GB * E)].rearrange("p (b e) -> p b e", e=E),
                                  ps[:, 2, 0:GB * E].rearrange("p (b e) -> p b e", e=E), rb, ALU.add).then_inc(lg_sb, 1)
            dve.wait_ge(lg_sb, NG)
            v3 = lambda z: z.rearrange("p (b e) -> p b e", e=E)
            b3 = lambda z: z.rearrange("p (b a) -> p b a", a=1).to_broadcast([P, NB, E])
            k3 = lambda z: z.rearrange("p (a e) -> p a e", a=1).to_broadcast([P, NB, E])
            dve.memset(rt[6], 1.0).then_inc(lgx, 1)
            dve.wait_ge(sig, 1)
            link(dve.tensor_scalar(lg, lg, 1.0, None, ALU.add))
            link(dve.reciprocal(lg, lg))
            prob = [lg, rt[3]]
            oh = [rt[1], rt[2]]
            for k in range(2):
                link(dve.tensor_reduce(mmax[k], v3(prob[k]), AX.X, ALU.max))
                link(dve.tensor_tensor(v3(rt[0]), v3(prob[k]), b3(mmax[k]), ALU.is_ge))
                link(dve.scalar_tensor_tensor(out=v3(rt[0]), in0=v3(rt[0]), scalar=-8.0, in1=k3(cst[:, K_I8:K_I8 + E]),
                                              op0=ALU.mult, op1=ALU.add))
                link(dve.tensor_reduce(imin[k], v3(rt[0]), AX.X, ALU.min))
                link(dve.tensor_tensor(v3(oh[k]), v3(rt[0]), b3(imin[k]), ALU.is_equal))
                if k == 0:
                    link(dve.scalar_tensor_tensor(out=rt[3], in0=oh[0], scalar=-4.0, in1=lg, op0=ALU.mult, op1=ALU.add))
            dve.tensor_tensor(rt[4], oh[0], oh[1], ALU.add).then_inc(oh_ready, 1)
            link(dve.tensor_tensor(t32, mmax[0], mmax[1], ALU.add))
            link(dve.reciprocal(t32, t32))
            for k in range(2):
                dve.tensor_tensor(w12[k], mmax[k], t32, ALU.mult)
            dve.wait_ge(rank_ps, 1)
            eb = lambda z: z.rearrange("p (b e) -> p e b", e=E)
            link(dve.tensor_copy(rt[5].rearrange("p (e b) -> p e b", e=E), eb(ps[:, 7, 0:NB * E])))
            link(dve.tensor_tensor_scan(rt[0], rt[6], rt[5], 0.0, ALU.mult, ALU.add))
            cum = rt[0].rearrange("p (e b) -> p e b", e=E)
            exc = rt[3].rearrange("p (e b) -> p e b", e=E)
            link(dve.tensor_tensor(rt[3], rt[0], rt[5], ALU.subtract))
            cnt, til, inc, off, st = e8
            link(dve.tensor_tensor(cnt, cum[:, :, NB - 1], exc[:, :, 0], ALU.subtract))
            link(dve.tensor_scalar(til, cnt, 127.0, 1.0 / 128.0, ALU.add, ALU.mult))
            link(dve.tensor_scalar(til, til, 127.0 / 256.0, MAGIC, ALU.subtract, ALU.add))
            link(dve.tensor_scalar(til, til, MAGIC, None, ALU.subtract))
            link(dve.tensor_tensor_scan(inc, rt[6][:, 0:E], til, 0.0, ALU.mult, ALU.add))
            link(dve.tensor_tensor(off, inc, til, ALU.subtract))
            link(dve.tensor_scalar(off, off, float(P), float(NB * P), ALU.mult, ALU.add))
            link(dve.tensor_tensor(st, off, exc[:, :, 0], ALU.subtract))
            link(dve.tensor_tensor(exc, exc, st.rearrange("p (e a) -> p e a", a=1).to_broadcast([P, E, NB]), ALU.add))
            link(dve.tensor_tensor(v3(rt[5]), v3(ps[:, 6, 0:NB * E]), rt[3].rearrange("p (e b) -> p b e", e=E), ALU.add))
            for k in range(2):
                link(dve.tensor_tensor(rt[0], oh[k], rt[5], ALU.mult))
                link(dve.tensor_reduce(slotf[k], v3(rt[0]), AX.X, ALU.add))
                link(dve.tensor_copy(slot_i[k], slotf[k]))
            tl = work[:, 3 * 256:3 * 256 + RT * E].rearrange("p (t e) -> p t e", e=E)
            link(dve.tensor_tensor(tl, cst[:, K_TILE:K_TILE + RT].rearrange("p (t a) -> p t a", a=1).to_broadcast([P, RT, E]),
                                   inc.rearrange("p (a e) -> p a e", a=1).to_broadcast([P, RT, E]), ALU.is_ge))
            link(dve.tensor_reduce(rt[0][:, 0:RT], tl, AX.X, ALU.add))
            link(dve.tensor_scalar(eidx, rt[0][:, 0:RT], float(E - 1), 6144.0, ALU.min, ALU.mult))
            dve.tensor_copy(XR[:, :, D + 1], cst[:, K_ROW:K_ROW + NB])
            dve.tensor_copy(XR[:, :, D], w12[0]).then_inc(slots_ready, 1)

            def x_lo(n, par):
                dve.wait_ge(t_hi, n + 1)
                if at_least(n, 2):
                    dve.wait_ge(u_ps, n - 1)
                dve.scalar_tensor_tensor(out=xl[par], in0=ps[:, 5, 0:D].rearrange("p (k t) -> p k t", k=KC), scalar=XSCALE,
                                         in1=xh[par], op0=ALU.mult, op1=ALU.subtract).then_inc(t_lo, 1)

            def slot_meta(n, par, loads):
                r = n - NB
                dve.wait_ge(xt_in[par], loads * 16)
                ow = mw[:, r:r + 1] if isinstance(r, int) else mw[:, ds(r, 1)]
                orow = mrow[:, r:r + 1] if isinstance(r, int) else mrow[:, ds(r, 1)]
                dve.tensor_scalar(ow, xt_[par][:, D:D + 1], ysc[:, 0:1], None, ALU.mult)
                dve.tensor_copy(orow, xt_[par][:, D + 1:D + 2]).then_inc(meta, 1)

            def tile_dve(i, par, phase, prev_phase):
                n = i * 2 + par
                if isinstance(n, int) and n == NB:
                    slot_meta(n, par, i + 1)
                if at_least(n, 1):
                    dve.wait_ge(h_hi, n)
                    if at_least(n, 3):
                        dve.wait_ge(y_ps, n - 2)
                    dve.tensor_tensor(hl[1 - par], ps[:, 4, :].rearrange("p (c t) -> p c t", c=IC), hh[1 - par], ALU.subtract).then_inc(h_lo, 1)
                if not (isinstance(n, int) and n + 1 >= NT):
                    x_lo(n + 1, 1 - par)
                if phase:
                    dve.wait_ge(u_ps, n + 1)
                    dve.wait_ge(silu, n + 1)
                    dve.scalar_tensor_tensor(out=hs[par], in0=ps[:, 2 * par + 1, :], scalar=cus[:, 0:1], in1=hs[par],
                                             op0=ALU.mult, op1=ALU.mult).then_inc(hid, 1)
                if phase == "slots" and not (isinstance(n, int) and n + 1 >= NT):
                    slot_meta(n + 1, 1 - par, i + par + 1)
                if prev_phase == "shared" and at_least(n, 1):
                    dve.wait_ge(y_ps, n)
                    z = xt(n - 1)
                    dve.scalar_tensor_tensor(out=z, in0=ps[:, 7 - par, 0:D], scalar=ysc[:, 0:1], in1=z,
                                               op0=ALU.mult, op1=ALU.add).then_inc(y_add, 1)

            x_lo(0, 0)
            run_tiles(dve, tile_dve)

        @block.tensor
        def _(pe):
            pe.wait_ge(c_in, 48)

            def transposes(a, g, pr):
                pe.wait_ge(a.xn, g + 1)
                for b in range(GB):
                    for k in range(KC):
                        last = pe.transpose(pair(pr)[:, k, b * P:(b + 1) * P], a.B.xn[:, b, k * P:(k + 1) * P], ident)
                last.then_inc(a.xnT_ps, 1)

            def project_T(a, w, src, pr, done):
                for c in range(KC):
                    for k in range(KC):
                        last = pe.matmul(pair(pr)[:, c, :], watt[:, w, k, c * P:(c + 1) * P], src[:, k, :],
                                         start=(k == 0), stop=(k == KC - 1))
                last.then_inc(done, 1)

            def project_v(a, pr):
                for b in range(GB):
                    for k in range(KC):
                        last = pe.matmul(pair(pr)[:, b // 2, (b % 2) * D:(b % 2 + 1) * D], a.B.ctxb[:, k, b * P:(b + 1) * P],
                                         watt[:, 2, k, :], start=(k == 0), stop=(k == KC - 1))
                last.then_inc(a.v_ps, 1)

            def attention0_pe(a, g, has_prev, has_next):
                pe.wait_ge(a.xnT, g + 1)
                if has_prev:
                    pe.wait_ge(a.v, g)
                project_T(a, 0, xnT, 0, a.q_ps)
                pe.wait_ge(ctx_in, 16 * g + 16)
                project_T(a, 1, ctxb, 1, a.k_ps)
                pe.wait_ge(a.q, g + 1)
                project_v(a, 0)
                if has_prev:
                    pe.wait_ge(a.pt, g)
                    for h in range(2):
                        for s in range(8):
                            b, j = 2 * h + s // NH0, s % NH0
                            last = pe.matmul(pair(2 + h)[:, 0, s * 64:(s + 1) * 64], BD[:, b * NH0 + j, :],
                                             v[:, b, j * 64:(j + 1) * 64], start=True, stop=True)
                        last.then_inc(a.pv_ps, 1)
                pe.wait_ge(a.k, g + 1)
                if has_next:
                    transposes(a, g + 1, 1)
                for h in range(2):
                    if has_prev:
                        pe.wait_ge(a.pv, 2 * g - 1 + h)
                    for s in range(8):
                        bb, jh, par = s // 4, (s // 2) % 2, s % 2
                        r = slice(64 * par, 64 * par + 64)
                        t = slice((2 * h + bb) * P, (2 * h + bb + 1) * P)
                        m = bb * 2 + jh
                        last = pe.matmul(pair(2 + h)[:, par, m * P:(m + 1) * P], qT[r, jh, t], kT[r, jh, t], start=True, stop=True)
                    last.then_inc(a.s_ps, 1)

            a = A0
            transposes(a, 0, 1)
            pe.wait_ge(wat_in, 16)
            attention0_pe(a, 0, False, True)
            with pe.Fori(1, NG - 1) as g:
                attention0_pe(a, g, True, True)
            attention0_pe(a, NG - 1, True, False)
            pe.wait_ge(wq_ready, 1)
            pe.wait_ge(a.v, NG)
            for f in range(FC):
                for k in range(KC):
                    last = pe.transpose(psb[:, k, f * P:(f + 1) * P], w1q[:, f, k * P:(k + 1) * P], identb)
            last.then_inc(wT_ps, 1)
            pe.wait_ge(a.pt, NG)
            for h in range(2):
                for s in range(8):
                    b, j = 2 * h + s // NH0, s % NH0
                    last = pe.matmul(pair(2 + h)[:, 0, s * 64:(s + 1) * 64], BD[:, b * NH0 + j, :],
                                     v[:, b, j * 64:(j + 1) * 64], start=True, stop=True)
                last.then_inc(a.pv_ps, 1)
            pe.wait_ge(a.k, NG)
            for f in range(FC):
                for c in range(2):
                    last = pe.transpose(psb[:, 2 + f // 4, (f % 4) * D + c * P:(f % 4) * D + (c + 1) * P],
                                        w2q[:, c, f * P:(f + 1) * P], identb)
            last.then_inc(wT_ps, 1)

            def transposes_q(g):
                pe.wait_ge(xq_b, g + 1)
                if isinstance(g, int) and g == 0:
                    pe.wait_ge(a.pv, 2 * NG)
                else:
                    pe.wait_ge(xqT_sb, g)
                for b in range(GB):
                    for k in range(KC):
                        last = pe.transpose(psb[:, 7, k * GT + b * P:k * GT + (b + 1) * P], xqb[:, b, k * P:(k + 1) * P], identb)
                last.then_inc(xqT_ps, 1)

            def hidden(g, q, pr, done):
                for f in range(2):
                    for k in range(KC):
                        rhs = XQT[:, k, ds(g * GT, GT)] if not isinstance(g, int) else XQT[:, k, g * GT:(g + 1) * GT]
                        last = pe.matmul(pair(pr)[:, f, :], w1T[:, k, (2 * q + f) * P:(2 * q + f + 1) * P], rhs,
                                         start=(k == 0), stop=(k == KC - 1))
                last.then_inc(done, 1)

            def pass_a(i, first, last_pair):
                for half in range(2):
                    gg = i * 2 + half
                    if not (last_pair and half):
                        transposes_q(gg + 1)
                    pe.wait_ge(xqT_sb, gg + 1)
                    for q in range(4):
                        n = 4 * half + q
                        if n >= 3:
                            pe.wait_ge(fa_max, i * 8 + n - 2)
                        elif not first:
                            pe.wait_ge(fa_max, i * 8 + (-1, 0, -2)[n])
                        hidden(gg, q, n % 3, fa_ps)

            transposes_q(0)
            pe.wait_ge(wT_sb, 2)
            pass_a(0, True, False)
            with pe.Fori(1, NG // 2 - 1) as i:
                pass_a(i, False, False)
            pass_a(NG // 2 - 1, False, True)

            def pass_b(i, first):
                for n in range(8):
                    if n >= 3:
                        pe.wait_ge(f1_act, i * 8 + n - 2)
                    elif n == 2 and not first:
                        pe.wait_ge(f2_ev, i * 2)
                    hidden(i * 2 + n // 4, n % 4, n % 3, f1_ps)
                for half in range(2):
                    pe.wait_ge(f1_q, i * 8 + 4 * half + 4)
                    if half:
                        pe.wait_ge(f1_act, i * 8 + 6)
                    for b in range(GB):
                        for f in range(FC):
                            last = pe.matmul(pair(3 - half)[:, b // 2, (b % 2) * D:(b % 2 + 1) * D],
                                             hq[half][:, f, b * P:(b + 1) * P], w2T[:, f, :], start=(f == 0), stop=(f == FC - 1))
                    last.then_inc(f2_ps, 1)

            pe.wait_ge(fa_max, 4 * NG)
            pass_b(0, True)
            with pe.Fori(1, NG // 2) as i:
                pass_b(i, False)

            def transpose_probs(a, g):
                pe.wait_ge(a.exp, g + 1)
                for b in range(GB):
                    last = pe.transpose(ps[:, 4, b * P:(b + 1) * P], S1[:, b, :], ident)
                last.then_inc(a.pt_ps, 1)

            def values(a, g):
                pe.wait_ge(a.pt, g + 1)
                if at_least(g, 1):
                    pe.wait_ge(a.pv, g)
                for b in range(GB):
                    last = pe.matmul(pair(3)[:, b // 2, (b % 2) * D:(b % 2 + 1) * D], PT[:, b, :], B1.v[:, b, :], start=True, stop=True)
                last.then_inc(a.pv_ps, 1)

            def attention1_pe(a, g, has_prev, has_next):
                pe.wait_ge(a.xnT, g + 1)
                if has_prev:
                    pe.wait_ge(a.v, g)
                project_T(a, 0, B1.xnT, 0, a.q_ps)
                pe.wait_ge(ctx1_in, 16 * g + 16)
                project_T(a, 1, B1.ctxb, 1, a.k_ps)
                pe.wait_ge(a.q, g + 1)
                project_v(a, 0)
                if has_prev:
                    transpose_probs(a, g - 1)
                    values(a, g - 1)
                pe.wait_ge(a.k, g + 1)
                if has_next:
                    transposes(a, g + 1, 1)
                if has_prev:
                    pe.wait_ge(a.s_sb, g)
                for b in range(GB):
                    for k in range(KC):
                        last = pe.matmul(ps[:, 5, b * P:(b + 1) * P], B1.qT[:, k, b * P:(b + 1) * P], B1.kT[:, k, b * P:(b + 1) * P],
                                         start=(k == 0), stop=(k == KC - 1))
                last.then_inc(a.s_ps, 1)

            a = A1
            pe.wait_ge(f2_ev, NG)
            pe.wait_ge(wat_in, 32)
            transposes(a, 0, 1)
            attention1_pe(a, 0, False, True)
            with pe.Fori(1, NG - 1) as g:
                attention1_pe(a, g, True, True)
            attention1_pe(a, NG - 1, True, False)
            transpose_probs(a, NG - 1)
            values(a, NG - 1)

            pe.wait_ge(wrt_in, 16)
            pe.wait_ge(a.v, NG)
            with pe.Fori(0, NG) as g:
                pe.wait_ge(xnb_ready, g + 1)
                for b in range(GB):
                    for k in range(KC):
                        last = pe.transpose(pair(0)[:, k, b * P:(b + 1) * P], xnb[:, b, k * P:(k + 1) * P], ident)
                last.then_inc(xnbT_ps, 1)
                pe.wait_ge(xnbT_sb, g + 1)
                for b in range(GB):
                    for k in range(KC):
                        last = pe.matmul(ps[:, 2, b * E:(b + 1) * E], xnbT[:, k, b * P:(b + 1) * P], wrts[:, k, :],
                                         start=(k == 0), stop=(k == KC - 1))
                last.then_inc(lg_ps, 1)
                pe.wait_ge(lg_sb, g + 1)
            pe.wait_ge(oh_ready, 1)
            pe.matmul(ps[:, 6, 0:NB * E], tri, rt[4], start=True, stop=True)
            pe.matmul(ps[:, 7, 0:NB * E], ones, rt[4], start=True, stop=True).then_inc(rank_ps, 1)

            def x_transpose(n, par, loads):
                pe.wait_ge(xt_in[par], loads * 16)
                if at_least(n, 1):
                    pe.wait_ge(t_lo, n)
                for k in range(KC):
                    last = pe.transpose(ps[:, 5, k * P:(k + 1) * P], xt_[par][:, k * P:(k + 1) * P], ident)
                last.then_inc(t_ps, 1)

            def weights(phase, r, off, width):
                if phase != "slots":
                    return lambda o: WM[:, E * 6144 + off + o:E * 6144 + off + o + width]
                tile = eidx[0:1, r:r + 1] if isinstance(r, int) else eidx[0:1, ds(r, 1)]
                e = pe.value_load(tile, min_val=0, max_val=(E - 1) * 6144)
                return lambda o: WM[:, ds(e + (off + o), width)]

            def tile_pe(i, par, phase, prev_phase):
                n = i * 2 + par
                if isinstance(n, int) and n == NB:
                    pe.wait_ge(slots_ready, 1)
                w_up = weights(phase, n - NB, 0, I)
                if at_least(n, 1):
                    pe.wait_ge(hid, n)
                    if at_least(n, 2):
                        pe.wait_ge(h_lo, n - 1)
                    for c in range(IC):
                        last = pe.transpose(ps[:, 4, c * P:(c + 1) * P], hs[1 - par][:, c * P:(c + 1) * P], ident)
                    last.then_inc(h_ps, 1)
                last_tile = isinstance(n, int) and n + 1 >= NT
                if phase:
                    pe.wait_ge(t_hi, n + 1)
                    pe.wait_ge(t_lo, n + 1)
                    for m, done in ((0, g_ps), (1, u_ps)):
                        z = ps[:, 2 * par + m, :]
                        for k in range(KC):
                            pe.matmul(z, xh[par][:, k, :], w_up(m * 2048 + k * I), start=(k == 0), stop=False)
                            pe.matmul(z, xh[par][:, k, :], w_up(m * 2048 + 1024 + k * I), start=False, stop=False)
                            last = pe.matmul(z, xl[par][:, k, :], w_up(m * 2048 + k * I), start=False, stop=(k == KC - 1))
                        last.then_inc(done, 1)
                        if m == 0 and not last_tile:
                            x_transpose(n + 1, 1 - par, i + par + 1)
                w_down = weights(prev_phase, n - (1 + NB), 4096, D)
                if at_least(n, 1):
                    pe.wait_ge(h_hi, n)
                    pe.wait_ge(h_lo, n)
                    if at_least(n, 3):
                        if prev_phase == "shared" or (isinstance(n, int) and n < NB + 3):
                            pe.wait_ge(y_add, n - 2)
                        else:
                            pe.wait_ge(y_sb, n - (2 + NB))
                    z = ps[:, 7 - par, 0:D]
                    for c in range(IC):
                        pe.matmul(z, hh[1 - par][:, c, :], w_down(c * D), start=(c == 0), stop=False)
                        pe.matmul(z, hh[1 - par][:, c, :], w_down(1024 + c * D), start=False, stop=False)
                        last = pe.matmul(z, hl[1 - par][:, c, :], w_down(c * D), start=False, stop=(c == IC - 1))
                    last.then_inc(y_ps, 1)

            x_transpose(0, 0, 1)
            pe.wait_ge(wlo, NE)
            run_tiles(pe, tile_pe)


_IN = ["x", "ctxT", "mask", "wqkv0", "wqkv1", "cols", "rows", "w1", "w2", "wmoe", "wrt", "consts"]


def kernel(**inputs):
    import concourse.bacc as bacc
    from concourse.bass_utils import run_bass_kernel_spmd

    a = {k: np.asarray(v) for k, v in inputs.items()}
    seq = lambda z: z.reshape(NB, 32, 4, D).transpose(0, 2, 1, 3).reshape(NB, P, D)
    wmat = lambda w: w.reshape(KC, P, D).transpose(1, 0, 2)
    col = lambda z: z.reshape(-1, P).T
    ctxs = seq(a["ctx_1024"])
    m = a["mask_BxSxS2_fk0"].reshape(NB, 32, 4, 32, 4).transpose(2, 1, 0, 4, 3).reshape(P, NB, P)
    up = lambda w: w.reshape(I, KC, P).transpose(2, 1, 0).reshape(P, KC * I)
    down = lambda w: w.reshape(D, IC, P).transpose(2, 1, 0).reshape(P, IC * D)
    moe = [[up(w) for w in (*a["L1_ffn_wg"], a["L1_ffn_sg_w"])], [up(w) for w in (*a["L1_ffn_wu"], a["L1_ffn_su_w"])],
           [down(w) for w in (*a["L1_ffn_wd"], a["L1_ffn_sd_w"])]]
    data = {
        "x": seq(a["x"]).transpose(1, 0, 2),
        "ctxT": ctxs.reshape(NG, GT, KC, P).transpose(3, 0, 2, 1),
        "mask": m,
        "wqkv0": np.stack([wmat(a[f"L0_xattn_W{n}"].T) for n in "qkv"], 1),
        "wqkv1": np.stack([wmat(a[f"L1_xattn_W{n}"]) for n in "qkv"], 1),
        "cols": np.concatenate([col(a[n]) for n in ("L0_xattn_bq", "L0_xattn_bk", "L1_xattn_bq", "L1_xattn_bk", "L0_ffn_b1")], 1),
        "rows": np.concatenate([a[n].reshape(-1) for n in ("L0_xattn_bv", "L1_xattn_bv", "L0_ffn_b2", "L1_ffn_routing_bias", "g_xattn", "g_ffn")])[None],
        "w1": a["L0_ffn_w1"].reshape(FC, P, D).transpose(1, 0, 2),
        "w2": a["L0_ffn_w2"].reshape(2, P, F).transpose(1, 0, 2),
        "wmoe": np.stack([np.stack(w, 1) for w in moe], 2),
        "wrt": a["L1_ffn_router_w"].T.reshape(KC, P, E).transpose(1, 0, 2),
        "consts": np.concatenate([np.eye(P), np.triu(np.ones((P, P)), 1), np.ones((P, P)), np.tile(np.arange(E) + 8.0, (P, 1)),
                                  np.arange(P * NB).reshape(P, NB), np.tile(np.arange(RT), (P, 1))], 1).astype(np.float32),
    }
    nc = bacc.Bacc("TRN2", target_bir_lowering=False, num_devices=1)
    arrays, args = {}, []
    for n in _IN:
        z = np.ascontiguousarray(data[n])
        arrays[n] = z
        args.append(nc.dram_tensor(n, z.shape, F32, kind="ExternalInput").ap())
    args.append(nc.dram_tensor("result", (P, NB, D), F32, kind="ExternalOutput").ap())
    bass_gated_two_layer(nc, *args)
    r = run_bass_kernel_spmd(nc, [arrays], core_ids=[0])
    y = r.results[0]["result"]
    return y.reshape(4, 32, NB, D).transpose(2, 1, 0, 3).reshape(NB, P, D)
```

```python
from contextlib import ExitStack

import numpy as np
import concourse.bass as bass
from concourse import mybir

F32 = mybir.dt.float32
F16 = mybir.dt.float16
BF16 = mybir.dt.bfloat16
I32 = mybir.dt.int32
ALU = mybir.AluOpType
ACT = mybir.ActivationFunctionType
AX = mybir.AxisListType
ds = bass.ds

P = 128
NB = 32
D = 256
KC = D // P
GB = 4
NG = NB // GB
GT = GB * P
NH0 = 4
BLK = 32
F = 1024
FC = F // P
E = 8
NE = E + 1
I = 512
IC = I // P
HALF = KC * I
MAT = 2 * HALF
WEXP = 3 * MAT
RT = 2 * NB + E - 1
SLOTS = RT * P
EPS = 1e-5
QEPS = 1e-8
MAGIC = 12582912.0
XSCALE = 256.0

C_BQ0, C_BK0, C_BQ1, C_BK1, C_B1 = 0, 2, 4, 6, 8
NCOL = 16
R_BV0, R_BV1, R_B2, R_RB, R_G = 0, 256, 512, 768, 776
NROW = R_G + 4
K_ID, K_TRI, K_ONE, K_I8, K_ROW, K_TILE = 0, 128, 256, 384, 392, 424
NCONST = 424 + RT
ROW = D + 2
NT = NB + RT
NO_ROW = 1.0e6


def at_least(n, k):
    return not isinstance(n, int) or n >= k


def run_tiles(eng, step):
    one = lambda n: step(n // 2, n % 2, None if n == NT else "shared" if n < NB else "slots", "shared" if n <= NB else "slots")
    for n in range(4):
        one(n)
    with eng.Fori(2, NB // 2) as i:
        step(i, 0, "shared", "shared")
        step(i, 1, "shared", "shared")
    for n in range(NB, NB + 4):
        one(n)
    with eng.Fori(NB // 2 + 2, NT // 2 - 1) as i:
        step(i, 0, "slots", "slots")
        step(i, 1, "slots", "slots")
    for n in range(NT // 2 * 2 - 2, NT + 1):
        one(n)


def counted(eng, value):
    if not isinstance(value, int):
        eng.compute_val(value)
    return value


class Chain:

    def __init__(self, eng, sem, base=0):
        self.eng, self.sem, self.base, self.n = eng, sem, base, 0

    def __call__(self, ins, held=None):
        self.n += 1
        ins.then_inc(self.sem, 1)
        count = counted(self.eng, self.base + self.n)
        if held is not None:
            self.eng.wait_ge(held, 1)
        self.eng.wait_ge(self.sem, count)


def bass_gated_two_layer(nc, x, ctxT, mask, wqkv0, wqkv1, cols, rows, w1, w2, wmoe, wrt, consts, out):
    ctx = ExitStack()
    with ctx:
        def sb(name, shape, dt=F32):
            return ctx.enter_context(nc.sbuf_tensor(name, shape, dt))

        def sem(name):
            return ctx.enter_context(nc.semaphore(name))

        X = sb("X", [P, NB, D])
        XNF = sb("XNF", [P, NB * ROW])
        XN = XNF[:, 0:NB * D].rearrange("p (b d) -> p b d", b=NB)
        XR = XNF[:, :].rearrange("p (b r) -> p b r", b=NB)
        WM_ELEMS = NE * WEXP
        WM = sb("WM", [P, WM_ELEMS], F16)
        WMF = WM[:, :].bitcast(F32)
        used = [0]

        def arena(n, dt=F32):
            a = WMF[:, used[0]:used[0] + n]
            used[0] += n
            assert used[0] <= WM_ELEMS // 2
            return a if dt == F32 else a.bitcast(dt)

        cst = sb("cst", [P, NCONST])
        ident = cst[:, K_ID:K_ID + P]
        ones = cst[:, K_ONE:K_ONE + P]
        tri = cst[:, K_TRI:K_TRI + P]
        colv = sb("colv", [P, NCOL])
        rowv = sb("rowv", [P, NROW])
        small = sb("small", [P, 1300])
        so = [0]

        def sm(n):
            a = small[:, so[0]:so[0] + n]
            so[0] += n
            assert so[0] <= 1300
            return a

        tg = sm(4)
        neghalf = sm(4)
        bnst = [sm(6 * GB), sm(6 * GB)]
        mv = [sm(2 * GB), sm(2 * GB)]
        ve = [sm(GB), sm(GB)]
        rs1 = sm(GB)
        nmr = sm(GB)
        rs2 = sm(NB)
        xmx = sm(NB)
        rmax = sm(16)
        rsum = sm(16)
        rinv = sm(16)
        t32 = sm(NB)
        g1 = sm(8)
        sc = sm(16)
        aq = sm(NB)
        cf = sm(FC)
        bf = sm(FC)
        ca = sm(FC)
        ba = sm(FC)
        hm = sm(FC)
        sw1 = sm(FC)
        iw1 = sm(FC)
        sw2 = sm(2)
        iw2 = sm(2)
        tf = sm(FC)

        wmx = sm(NE * 3)
        wm3 = sm(3)
        wa3 = sm(3)
        pw3 = sm(3)
        ip3 = sm(3)
        wsc = sm(3)
        cgs = sm(1)
        cus = sm(1)
        ysc = sm(1)
        negmax = sm(GB)
        mu4 = sm(NB)
        nm4 = sm(NB)
        w12 = [sm(NB), sm(NB)]
        mmax = [sm(NB), sm(NB)]
        imin = sm(NB)
        wsum = sm(NB)
        slotf = [sm(NB), sm(NB)]
        e8 = [sm(E) for _ in range(5)]
        rt8 = sm(ROW)
        oidx = [sm(1).bitcast(I32), sm(1).bitcast(I32)]

        WORK = 6144
        work = sb("work", [P, WORK])
        watt = work[:, 0:3 * KC * D].rearrange("p (w k d) -> p w k d", w=3, k=KC)
        wst = work[:, 1536:1536 + 3 * HALF]
        PT = work[:, 4608:5120].rearrange("p (b q) -> p b q", b=GB)
        rt = [work[:, 256 * n:256 * (n + 1)] for n in range(8)]
        lg = rt[7]
        left = work[:, 5120:5376]
        pick = work[:, 5376:5632]
        xnb = [work[:, o:o + 1024].rearrange("p (b d) -> p b d", b=GB) for o in (2048, 0)]
        xnbT = work[:, 3072:4096].rearrange("p (k t) -> p k t", k=KC)
        wrts = work[:, 5696:5696 + KC * E].rearrange("p (k e) -> p k e", k=KC)
        slot_i = [work[:, 5712 + NB * k:5712 + NB * (k + 1)].bitcast(I32) for k in range(2)]
        eidx = work[:, 5776:5776 + RT].bitcast(I32)
        mw = rt[0][:, 0:RT]
        mrow = rt[1][:, 0:RT].bitcast(I32)
        wo = [2048]

        def tw(n, dt=F32):
            w = work[:, wo[0]:wo[0] + n]
            wo[0] += n
            assert wo[0] <= 5696
            return w if dt == F32 else w.bitcast(dt)

        xt_ = [tw(ROW) for _ in range(2)]
        xh = [tw(KC * P // 2, F16).rearrange("p (k t) -> p k t", k=KC) for _ in range(2)]
        xl = [tw(KC * P // 2, F16).rearrange("p (k t) -> p k t", k=KC) for _ in range(2)]
        hs = [tw(I) for _ in range(2)]
        hh = [tw(I // 2, F16).rearrange("p (c t) -> p c t", c=IC) for _ in range(2)]
        hl = [tw(I // 2, F16).rearrange("p (c t) -> p c t", c=IC) for _ in range(2)]
        yb = [tw(D) for _ in range(2)]

        class Buffers:

            def __init__(s, words):
                s.ctxb = words(KC * GT).rearrange("p (k t) -> p k t", k=KC)
                s.xn = words(GB * D).rearrange("p (b d) -> p b d", b=GB)
                s.xnT = words(KC * GT).rearrange("p (k t) -> p k t", k=KC)
                s.qT = words(KC * GT).rearrange("p (k t) -> p k t", k=KC)
                s.kT = words(KC * GT).rearrange("p (k t) -> p k t", k=KC)
                s.v = words(GB * D).rearrange("p (b d) -> p b d", b=GB)
                s.S = words(512)
                s.otmp = words(GB * D).rearrange("p (b d) -> p b d", b=GB)

        B0 = Buffers(arena)
        ctxb, xn, xnT, qT, kT, v, otmp = B0.ctxb, B0.xn, B0.xnT, B0.qT, B0.kT, B0.v, B0.otmp
        S = B0.S.rearrange("p (s k) -> p s k", k=BLK)
        xw = [0]

        def xarena(n):
            a = XNF[:, xw[0]:xw[0] + n]
            xw[0] += n
            assert xw[0] <= NB * ROW
            return a

        B1 = Buffers(xarena)
        S1 = B1.S.rearrange("p (b k) -> p b k", b=GB)
        mk = xarena(GB * P).rearrange("p (b k) -> p b k", b=GB)
        BD = arena(16 * P).rearrange("p (s q) -> p s q", s=16)
        XQT = arena(NB * P * KC // 2, BF16).rearrange("p (k t) -> p k t", k=KC)
        hfm = arena(4 * GT)
        hf = [hfm[:, 2 * GT * n:2 * GT * (n + 1)].rearrange("p (a t) -> p a t", a=2) for n in range(2)]
        w1f = hfm.rearrange("p (f d) -> p f d", f=FC)
        hqm = [arena(FC * GT // 2) for _ in range(2)]
        hq = [z.bitcast(BF16).rearrange("p (f t) -> p f t", f=FC) for z in hqm]
        w2f = hqm[0].rearrange("p (c f) -> p c f", c=2)
        w1q = arena(FC * D // 2, BF16).rearrange("p (f d) -> p f d", f=FC)
        w2q = arena(2 * F // 2, BF16).rearrange("p (c f) -> p c f", c=2)
        w1T = arena(KC * F // 2, BF16).rearrange("p (k f) -> p k f", k=KC)
        w2T = arena(FC * D // 2, BF16).rearrange("p (f d) -> p f d", f=FC)
        identb = arena(P // 2, BF16)
        mxA = arena(NG * FC).rearrange("p (g f) -> p g f", g=NG)
        crow, brow, swrow, trow = (work[:, 5120 + D * n:5120 + D * (n + 1)] for n in range(4))
        assert used[0] <= E * WEXP // 2
        xqf = B0.xn
        xqb = B0.qT.rearrange("p k t -> p (k t)")[:, 0:GB * D // 2].bitcast(BF16).rearrange("p (b d) -> p b d", b=GB)

        ps = ctx.enter_context(nc.psum_tensor("ps", [P, 8, 512], F32))
        psb = ps[:, :, :].bitcast(BF16)

        def pair(n):
            return ps[:, 2 * n:2 * n + 2, :]

        xs_dram = nc.dram_tensor("dispatched", (SLOTS, ROW), F32).ap()
        sw_dram = nc.dram_tensor("sw2_scratch", (1, D), F32).ap()

        x_in = [sem(f"x_in{i}") for i in range(3)]
        c_in = sem("c_in")
        wat_in = sem("wat_in")
        ctx_in = sem("ctx_in")
        w12_in = sem("w12_in")
        dchain = sem("dchain")
        mset = sem("mset")
        tg_ready = sem("tg_ready")

        class L:
            def __init__(s, n, buffers):
                s.B = buffers
                s.ve1 = sem(f"a{n}_ve1")
                s.rstd1 = sem(f"a{n}_rstd1")
                s.nmr = sem(f"a{n}_nmr")
                s.xn = sem(f"a{n}_xn")
                s.xnT_ps = sem(f"a{n}_xnT_ps")
                s.xnT = sem(f"a{n}_xnT")
                s.q_ps = sem(f"a{n}_q_ps")
                s.q = sem(f"a{n}_q")
                s.k_ps = sem(f"a{n}_k_ps")
                s.k = sem(f"a{n}_k")
                s.v_ps = sem(f"a{n}_v_ps")
                s.v = sem(f"a{n}_v")
                s.s_ps = sem(f"a{n}_s_ps")
                s.s_sb = sem(f"a{n}_s_sb")
                s.sub = sem(f"a{n}_sub")
                s.exp = sem(f"a{n}_exp")
                s.pt_ps = sem(f"a{n}_pt_ps")
                s.pt = sem(f"a{n}_pt")
                s.pv_ps = sem(f"a{n}_pv_ps")
                s.pv = sem(f"a{n}_pv")
                s.res = sem(f"a{n}_res")
                s.ve2 = sem(f"a{n}_ve2")
                s.rstd2 = sem(f"a{n}_rstd2")
                s.d = sem(f"a{n}_d")

        A0, A1 = L(0, B0), L(1, B1)

        centred = sem("centred")
        xmx_done = sem("xmx_done")
        gm_ready = sem("gm_ready")
        gm_all = sem("gm_all")
        aq_ready = sem("aq_ready")
        xq_f = sem("xq_f")
        xq_b = sem("xq_b")
        xqT_ps = sem("xqT_ps")
        xqT_sb = sem("xqT_sb")
        wq_ready = sem("wq_ready")
        wT_ps = sem("wT_ps")
        wT_sb = sem("wT_sb")
        sw2_sb = sem("sw2_sb")
        sw2_st = sem("sw2_st")
        swrow_in = sem("swrow_in")
        fa_ps = sem("fa_ps")
        fa_max = sem("fa_max")
        hm_ready = sem("hm_ready")
        hm_all = sem("hm_all")
        cb_ready = sem("cb_ready")
        f1_ps = sem("f1_ps")
        f1_act = sem("f1_act")
        f1_q = sem("f1_q")
        f2_ps = sem("f2_ps")
        f2_ev = sem("f2_ev")
        f2_a = sem("f2_a")
        f2_res = sem("f2_res")

        ctx1_in, mask_in = sem("ctx1_in"), sem("mask_in")
        mneg = sem("mneg")
        nmx = sem("nmx")
        wst_in = sem("wst_in")
        wmax_done = sem("wmax_done")
        wm_ready = sem("wm_ready")
        wm_all = sem("wm_all")
        wsc_ready = sem("wsc_ready")
        whi = sem("whi")
        wlo = sem("wlo")

        nm4_ready = sem("nm4_ready")
        xnb_ready = sem("xnb_ready")
        xr_copied = sem("xr_copied")
        xnbT_ps = sem("xnbT_ps")
        xnbT_sb = sem("xnbT_sb")
        wrt_in = sem("wrt_in")
        lg_ps = sem("lg_ps")
        lg_sb = sem("lg_sb")
        sig = sem("sig")
        oh_ready = sem("oh_ready")
        rank_ps = sem("rank_ps")
        rank_sb = sem("rank_sb")
        slots_ready = sem("slots_ready")
        fill_ready, fill_st = sem("fill_ready"), sem("fill_st")
        w2_ready = sem("w2_ready")
        sent = sem("sent")

        xt_in = [sem("xt_in0"), sem("xt_in1")]
        t_ps = sem("t_ps")
        t_hi = sem("t_hi")
        t_lo = sem("t_lo")
        g_ps, u_ps = sem("g_ps"), sem("u_ps")
        silu = sem("silu")
        hid = sem("hid")
        h_ps = sem("h_ps")
        h_hi = sem("h_hi")
        h_lo = sem("h_lo")
        y_ps = sem("y_ps")
        y_add = sem("y_add")
        meta = sem("meta")
        y_sb = sem("y_sb")
        oidx_ready = sem("oidx_ready")
        out_st = sem("out_st")
        y_out = sem("y_out")

        block = ctx.enter_context(nc.Block())

        def xg(g):
            return X[:, ds(g * GB, GB), :] if not isinstance(g, int) else X[:, g * GB:(g + 1) * GB, :]

        def xt(t):
            return X[:, ds(t, 1), :].rearrange("p a d -> p (a d)") if not isinstance(t, int) else X[:, t, :]

        @block.sync
        def _(sp):
            sp.dma_start(X[:, 0:GB, :], x[:, 0:GB, :]).then_inc(x_in[0], 16)
            sp.dma_start(watt[:, :, :, :], wqkv0).then_inc(wat_in, 16)
            sp.dma_start(ctxb[:, :, :], ctxT[:, 0]).then_inc(ctx_in, 16)
            sp.dma_start(cst[:, :], consts).then_inc(c_in, 16)
            sp.dma_start(colv[:, :], cols).then_inc(c_in, 16)
            sp.dma_start(rowv[:, :], rows.partition_broadcast(P)).then_inc(c_in, 16)
            sp.dma_start(X[:, GB:2 * GB, :], x[:, GB:2 * GB, :]).then_inc(x_in[1], 16)
            sp.dma_start(w1f[:, :, :], w1).then_inc(w12_in, 16)
            sp.dma_start(w2f[:, :, :], w2).then_inc(w12_in, 16)
            sp.dma_start(X[:, 2 * GB:NB, :], x[:, 2 * GB:NB, :]).then_inc(x_in[2], 16)
            sp.dma_start(wst, wmoe[:, 0].rearrange("p m w -> p (m w)")).then_inc(wst_in, 16)
            with sp.Fori(1, NG) as g:
                sp.wait_ge(A0.v_ps, g)
                sp.dma_start(ctxb[:, :, :], ctxT[:, ds(g, 1)].rearrange("p a k t -> p (a k) t")).then_inc(ctx_in, 16)
                sp.wait_ge(wmax_done, g)
                sp.dma_start(wst, wmoe[:, ds(g, 1)].rearrange("p a m w -> p (a m w)")).then_inc(wst_in, 16)
            sp.wait_ge(wmax_done, NG)
            sp.dma_start(wst, wmoe[:, NG].rearrange("p m w -> p (m w)")).then_inc(wst_in, 16)
            sp.wait_ge(A0.v_ps, NG)
            sp.dma_start(watt, wqkv1).then_inc(wat_in, 16)
            sp.wait_ge(sw2_sb, 1)
            sp.dma_start(sw_dram.rearrange("a (p c) -> p (a c)", p=P), sw2).then_inc(sw2_st, 16)
            sp.wait_ge(sw2_st, 16)
            sp.dma_start(swrow, sw_dram.partition_broadcast(P)).then_inc(swrow_in, 16)
            sp.wait_ge(fill_ready, 1)
            sp.dma_start(xs_dram.rearrange("(t p) r -> p t r", p=P),
                         rt8.rearrange("p (a r) -> p a r", a=1).to_broadcast([P, RT, ROW])).then_inc(fill_st, 16)
            sp.wait_ge(wlo, 1)
            sp.dma_start(wst, wmoe[:, 0].rearrange("p m w -> p (m w)")).then_inc(wst_in, 16)
            sp.wait_ge(xq_f, NG)
            sp.dma_start(B1.ctxb, ctxT[:, 0]).then_inc(ctx1_in, 16)
            sp.dma_start(mk, mask[:, 0:GB, :]).then_inc(mask_in, 16)
            with sp.Fori(1, NG) as g:
                sp.wait_ge(A1.v_ps, g)
                sp.dma_start(B1.ctxb, ctxT[:, ds(g, 1)].rearrange("p a k t -> p (a k) t")).then_inc(ctx1_in, 16)
                sp.wait_ge(wlo, g + 1)
                sp.dma_start(wst, wmoe[:, ds(g, 1)].rearrange("p a m w -> p (a m w)")).then_inc(wst_in, 16)
                sp.wait_ge(A1.s_sb, g)
                sp.dma_start(mk, mask[:, ds(g * GB, GB), :]).then_inc(mask_in, 16)
            sp.wait_ge(wlo, NE)
            sp.dma_start(wrts, wrt).then_inc(wrt_in, 16)

            def load_tile(n, par, phase):
                if at_least(n, 2):
                    count = counted(sp, n - 1)
                    sp.wait_ge(x_in[0], 16)
                    sp.wait_ge(t_ps, count)
                if phase == "shared":
                    src = XR[:, n, 0:D] if isinstance(n, int) else XR[:, ds(n, 1), 0:D].rearrange("p a d -> p (a d)")
                    sp.dma_start(xt_[par][:, 0:D], src).then_inc(xt_in[par], 16)
                else:
                    r = n - NB
                    if at_least(r, 2):
                        sp.wait_ge(meta, r - 1)
                    src = xs_dram[r * P:(r + 1) * P, :] if isinstance(r, int) else xs_dram[ds(r * P, P), :]
                    sp.dma_start(xt_[par][:, :], src).then_inc(xt_in[par], 16)

            sp.wait_ge(lg_sb, NG)
            for n in range(4):
                load_tile(n, n % 2, "shared")
            with sp.Fori(2, NB // 2) as i:
                load_tile(i * 2, 0, "shared")
                load_tile(i * 2 + 1, 1, "shared")
                sp.wait_ge(y_add, i * 2 - 2)
                sp.dma_start(out[:, ds(i * 2 - 4, 2), :], X[:, ds(i * 2 - 4, 2), :]).then_inc(out_st, 16)
            sp.wait_ge(sent, 16 * 2 * NB)
            for n in range(NB, NB + 4):
                load_tile(n, n % 2, "slots")
            sp.wait_ge(y_add, NB)
            sp.dma_start(out[:, NB - 4:NB, :], X[:, NB - 4:NB, :]).then_inc(out_st, 16)
            with sp.Fori(NB // 2 + 2, NT // 2) as i:
                load_tile(i * 2, 0, "slots")
                load_tile(i * 2 + 1, 1, "slots")
            for n in range(NT // 2 * 2, NT):
                load_tile(n, n % 2, "slots")

        @block.gpsimd
        def _(pool):
            pool.wait_ge(mset, 1)

            def attention_pool(a, g, has_prev, has_next2, npv, stats, add=True):
                if has_prev and add:
                    count = counted(pool, npv * g)
                    pool.wait_ge(mset, 1)
                    pool.wait_ge(a.pv, count)
                    pool.tensor_tensor(xg(g - 1), xg(g - 1), a.B.otmp, ALU.add).then_inc(a.res, 1)
                if has_next2:
                    count = counted(pool, g + 3)
                    pool.wait_ge(mset, 1)
                    pool.wait_ge(a.ve1, count)
                    pool.wait_ge(a.xn, g + 2)
                    pool.tensor_tensor(rs1, ve[0], neghalf, ALU.pow).then_inc(a.rstd1, 1)
                if has_prev:
                    count = counted(pool, g)
                    pool.wait_ge(mset, 1)
                    pool.wait_ge(a.ve2, count)
                    pool.tensor_tensor(stats[:, ds(g * GB - GB, GB)] if not isinstance(g, int) else
                                       stats[:, (g - 1) * GB:g * GB], ve[1], neghalf, ALU.pow).then_inc(a.rstd2, 1)

            a = A0
            for g in range(2):
                pool.wait_ge(a.ve1, g + 1)
                if g:
                    pool.wait_ge(a.xn, g)
                pool.tensor_tensor(rs1, ve[0], neghalf, ALU.pow).then_inc(a.rstd1, 1)
            attention_pool(a, 0, False, True, 2, rs2)
            with pool.Fori(1, NG - 2) as g:
                attention_pool(a, g, True, True, 2, rs2)
            attention_pool(a, NG - 2, True, False, 2, rs2)
            attention_pool(a, NG - 1, True, False, 2, rs2)
            attention_pool(a, NG, True, False, 2, rs2, add=False)

            pool.wait_ge(gm_ready, 1)
            pool.partition_all_reduce(g1[:, 1:2], g1[:, 0:1], P, bass.bass_isa.ReduceOp.max).then_inc(gm_all, 1)
            pool.wait_ge(wm_ready, 1)
            pool.partition_all_reduce(wa3, wm3, P, bass.bass_isa.ReduceOp.max).then_inc(wm_all, 1)
            pool.wait_ge(hm_ready, 1)
            pool.partition_all_reduce(g1[:, 3:4], g1[:, 2:3], P, bass.bass_isa.ReduceOp.max).then_inc(hm_all, 1)
            bb = brow.rearrange("p (a d) -> p a d", a=1).to_broadcast([P, GB, D])

            def residual(g):
                count = counted(pool, g + 1)
                pool.wait_ge(mset, 1)
                pool.wait_ge(f2_ev, count)
                pool.tensor_tensor(xg(g), xg(g), otmp, ALU.add).then_inc(f2_a, 1)
                count = counted(pool, g + 1)
                pool.wait_ge(mset, 1)
                pool.wait_ge(f2_a, count)
                pool.tensor_tensor(xg(g), xg(g), bb, ALU.add).then_inc(f2_res, 1)

            with pool.Fori(0, NG - 1) as g:
                residual(g)
            pool.wait_ge(A1.ve1, 1)
            pool.tensor_tensor(rs1, ve[0], neghalf, ALU.pow).then_inc(A1.rstd1, 1)
            residual(NG - 1)

            def negate_mask(g):
                count = counted(pool, 16 * g + 16)
                pool.wait_ge(mset, 1)
                pool.wait_ge(mask_in, count)
                pool.tensor_scalar(mk, mk, -1.0e9, None, ALU.mult).then_inc(mneg, 1)

            a = A1
            pool.wait_ge(a.ve1, 2)
            pool.wait_ge(a.xn, 1)
            pool.tensor_tensor(rs1, ve[0], neghalf, ALU.pow).then_inc(a.rstd1, 1)
            negate_mask(0)
            attention_pool(a, 0, False, True, 1, rs2)
            with pool.Fori(1, NG - 2) as g:
                negate_mask(g)
                attention_pool(a, g, True, True, 1, rs2)
            for g in (NG - 2, NG - 1):
                negate_mask(g)
                attention_pool(a, g, True, False, 1, rs2)
            attention_pool(a, NG, True, False, 1, rs2)

            pool.wait_ge(slots_ready, 1)
            pool.wait_ge(fill_st, 16)
            for k in range(2):
                if k:
                    pool.wait_ge(sent, 16 * NB)
                    pool.tensor_copy(XR[:, :, D], w12[1]).then_inc(w2_ready, 1)
                    pool.wait_ge(w2_ready, 1)
                for t in range(NB):
                    pool.indirect_dma_start(out=xs_dram, out_offset=bass.IndirectOffsetOnAxis(ap=slot_i[k][:, t:t + 1].bitcast(mybir.dt.uint32), axis=0),
                                            in_=XR[:, t, :], in_offset=None, bounds_check=SLOTS - 1, oob_is_err=False).then_inc(sent, 16)
            out_rows = out.rearrange("p b d -> (p b) d")
            pool.wait_ge(out_st, 16 * (NB // 2 - 1))

            def add_rows(r, par, first):
                count = counted(pool, r + 1)
                pool.wait_ge(mset, 1)
                pool.wait_ge(meta, count)
                src = mrow[:, r:r + 1] if isinstance(r, int) else mrow[:, ds(r, 1)]
                pool.tensor_copy(oidx[par], src).then_inc(oidx_ready, 1)
                pool.wait_ge(oidx_ready, r + 1)
                pool.wait_ge(y_sb, r + 1)
                if not first:
                    count = counted(pool, r * 16)
                    pool.wait_ge(mset, 1)
                    pool.wait_ge(y_out, count)
                pool.indirect_dma_start(out=out_rows, out_offset=bass.IndirectOffsetOnAxis(ap=oidx[par].bitcast(mybir.dt.uint32), axis=0),
                                        in_=yb[par], in_offset=None, bounds_check=NB * P - 1, oob_is_err=False,
                                        compute_op=ALU.add).then_inc(y_out, 16)

            add_rows(0, 0, True)
            add_rows(1, 1, False)
            with pool.Fori(1, RT // 2) as i:
                add_rows(i * 2, 0, False)
                add_rows(i * 2 + 1, 1, False)
            for r in range(RT // 2 * 2, RT):
                add_rows(r, r % 2, False)
            pool.wait_ge(y_out, 16 * RT)

        @block.scalar
        def _(act):
            def normalise(a, g):
                act.wait_ge(a.nmr, g + 1)
                if not (isinstance(g, int) and g == 0):
                    act.wait_ge(a.xnT_ps, g)
                for b in range(GB):
                    src = xt(g * GB + b)
                    last = act.activation(a.B.xn[:, b, :], src, ACT.Identity, bias=nmr[:, b:b + 1], scale=rs1[:, b:b + 1])
                last.then_inc(a.xn, 1)

            def evac_xnT(a, g, pr):
                act.wait_ge(a.xnT_ps, g + 1)
                act.activation(a.B.xnT, pair(pr), ACT.Copy).then_inc(a.xnT, 1)

            def evac_proj(ps_sem, sb_sem, dst, pr, col, g, free_sem):
                act.wait_ge(ps_sem, g + 1)
                if free_sem is not None:
                    act.wait_ge(free_sem[0], free_sem[1])
                for c in range(KC):
                    last = act.activation(dst[:, c, :], pair(pr)[:, c, :], ACT.Identity, bias=colv[:, col + c:col + c + 1])
                last.then_inc(sb_sem, 1)

            def attention0_act(a, g, has_prev, has_next):
                free = (a.s_ps, 2 * g) if has_prev else None
                evac_proj(a.q_ps, a.q, qT, 0 if has_prev else 3, C_BQ0, g, free)
                if has_prev:
                    if has_next:
                        normalise(a, g + 1)
                    evac_proj(a.k_ps, a.k, kT, 1, C_BK0, g, None)
                if has_next:
                    evac_xnT(a, g + 1, 1)
                if has_prev:
                    act.wait_ge(a.pt, g)
                for h in range(2):
                    act.wait_ge(a.s_ps, 2 * g + h + 1)
                    for c in range(4):
                        r = slice(BLK * c, BLK * (c + 1))
                        dst = S[r, 8 * h:8 * h + 8, :].rearrange("p (m a) k -> p a m k", a=2)
                        src = pair(2 + h)[r, :, :].rearrange("p a (m q) -> p a m q", m=4)[:, :, :, r]
                        for par in range(2):
                            last = act.activation(dst[:, par], src[:, par], ACT.Copy)
                    last.then_inc(a.s_sb, 1)
                act.wait_ge(a.sub, g + 1)
                act.activation(S[:, :, :], S[:, :, :], ACT.Exp, scale=0.125).then_inc(a.exp, 1)

            a = A0
            normalise(a, 0)
            act.wait_ge(c_in, 48)
            act.activation(tg, rowv[:, R_G:R_G + 4], ACT.Tanh).then_inc(tg_ready, 1)
            evac_proj(a.k_ps, a.k, kT, 1, C_BK0, 0, None)
            evac_xnT(a, 0, 2)
            normalise(a, 1)
            attention0_act(a, 0, False, True)
            with act.Fori(1, NG - 1) as g:
                attention0_act(a, g, True, True)
            attention0_act(a, NG - 1, True, False)

            act.wait_ge(aq_ready, 1)

            def scale_rows(g):
                if at_least(g, 1):
                    act.wait_ge(xq_b, g)
                for b in range(GB):
                    t = g * GB + b
                    src = XN[:, t, :] if isinstance(t, int) else XN[:, ds(t, 1), :].rearrange("p a d -> p (a d)")
                    last = act.activation(xqf[:, b, :], src, ACT.Identity, bias=sc[:, 8:9],
                                          scale=aq[:, t:t + 1] if isinstance(t, int) else aq[:, ds(t, 1)])
                last.then_inc(xq_f, 1)

            def round_rows(g):
                act.wait_ge(xq_f, g + 1)
                act.activation(xqb, xqf, ACT.Relu, bias=sc[:, 9:10]).then_inc(xq_b, 1)

            def evac_rows(g):
                act.wait_ge(xqT_ps, g + 1)
                dst = XQT[:, :, g * GT:(g + 1) * GT] if isinstance(g, int) else XQT[:, :, ds(g * GT, GT)]
                act.activation(dst, psb[:, 7, :].rearrange("p (k t) -> p k t", k=KC), ACT.Copy).then_inc(xqT_sb, 1)

            scale_rows(0)
            round_rows(0)
            with act.Fori(0, NG - 1) as g:
                scale_rows(g + 1)
                evac_rows(g)
                round_rows(g + 1)
            evac_rows(NG - 1)

            def split_hi(e, parts=(0, 1, 2)):
                if isinstance(e, int) and e == E:
                    act.wait_ge(wst_in, NE * 16)
                else:
                    act.wait_ge(wst_in, e * 16 + (NE + 1) * 16)
                for m in parts:
                    off = e * WEXP + m * MAT
                    dst = WM[:, ds(off, HALF)] if not isinstance(e, int) else WM[:, off:off + HALF]
                    act.activation(dst, wst[:, m * HALF:(m + 1) * HALF], ACT.Identity, scale=wsc[:, m:m + 1]).then_inc(whi, 1)

            act.wait_ge(wsc_ready, 1)
            split_hi(E)

            act.wait_ge(cb_ready, 1)

            def hidden_act(i, first):
                for n in range(8):
                    act.wait_ge(f1_ps, i * 8 + n + 1)
                    if n >= 2 or not first:
                        act.wait_ge(f1_q, i * 8 + n - 1)
                    for k in range(2):
                        f = 2 * (n % 4) + k
                        last = act.activation(hf[n % 2][:, k, :], pair(n % 3)[:, k, :], ACT.Relu,
                                              bias=ba[:, f:f + 1], scale=ca[:, f:f + 1])
                    last.then_inc(f1_act, 1)

            hidden_act(0, True)
            with act.Fori(1, NG // 2) as i:
                hidden_act(i, False)

            def attention1_act(a, g, has_prev, has_next):
                free = (a.s_ps, g) if has_prev else None
                evac_proj(a.q_ps, a.q, B1.qT, 0, C_BQ1, g, free)
                split_hi(g, (0, 1))
                if has_next:
                    normalise(a, g + 1)
                evac_proj(a.k_ps, a.k, B1.kT, 1, C_BK1, g, None)
                if has_prev:
                    act.wait_ge(a.pt_ps, g)
                    act.activation(PT, ps[:, 4, :].rearrange("p (b q) -> p b q", b=GB), ACT.Copy).then_inc(a.pt, 1)
                split_hi(g, (2,))
                if has_next:
                    evac_xnT(a, g + 1, 1)
                act.wait_ge(nmx, g + 1)
                if has_prev:
                    act.wait_ge(a.sub, g)
                for b in range(GB):
                    last = act.activation(S1[:, b, :], S1[:, b, :], ACT.Exp, bias=negmax[:, b:b + 1], accum_out=rsum[:, b:b + 1])
                last.then_inc(a.exp, 1)

            a = A1
            normalise(a, 0)
            evac_xnT(a, 0, 1)
            attention1_act(a, 0, False, True)
            with act.Fori(1, NG - 1) as g:
                attention1_act(a, g, True, True)
            attention1_act(a, NG - 1, True, False)
            act.wait_ge(a.pt_ps, NG)
            act.activation(PT, ps[:, 4, :].rearrange("p (b q) -> p b q", b=GB), ACT.Copy).then_inc(a.pt, 1)

            def router_norm(g, par):
                if at_least(g, 2):
                    act.wait_ge(xr_copied, g - 1)
                    act.wait_ge(xnbT_ps, g - 1)
                for b in range(GB):
                    t = g * GB + b
                    bias, scale = (z[:, t:t + 1] if isinstance(t, int) else z[:, ds(t, 1)] for z in (nm4, rs2))
                    last = act.activation(xnb[par][:, b, :], xt(t), ACT.Identity, bias=bias, scale=scale)
                last.then_inc(xnb_ready, 1)

            def router_evac(g, par):
                act.wait_ge(xnbT_ps, g + 1)
                if at_least(g, 1):
                    act.wait_ge(lg_ps, g)
                act.activation(xnbT, pair(par), ACT.Copy).then_inc(xnbT_sb, 1)

            def router_exp(g0, g1):
                act.wait_ge(lg_sb, g1)
                z = lg[:, g0 * GB * E:g1 * GB * E]
                act.activation(z, z, ACT.Exp, scale=-1.0).then_inc(sig, 1)

            act.wait_ge(wlo, NE)
            act.wait_ge(nm4_ready, 1)
            router_norm(0, 0)
            router_norm(1, 1)
            router_evac(0, 0)
            with act.Fori(1, NG // 2 - 1) as i:
                router_norm(i * 2, 0)
                router_evac(i * 2 - 1, 1)
                router_norm(i * 2 + 1, 1)
                router_evac(i * 2, 0)
            router_norm(NG - 2, 0)
            router_evac(NG - 3, 1)
            act.wait_ge(nm4_ready, 2)
            router_norm(NG - 1, 1)
            router_evac(NG - 2, 0)
            router_exp(0, NG - 2)
            router_evac(NG - 1, 1)
            router_exp(NG - 2, NG)

            def x_hi(n, par):
                act.wait_ge(t_ps, n + 1)
                if at_least(n, 2):
                    act.wait_ge(u_ps, n - 1)
                act.activation(xh[par], ps[:, 5, 0:D].rearrange("p (k t) -> p k t", k=KC), ACT.Copy, scale=XSCALE).then_inc(t_hi, 1)

            def tile_act(i, par, phase, prev_phase):
                n = i * 2 + par
                if at_least(n, 1):
                    act.wait_ge(h_ps, n)
                    if at_least(n, 3):
                        act.wait_ge(y_ps, n - 2)
                    act.activation(hh[1 - par], ps[:, 4, :].rearrange("p (c t) -> p c t", c=IC), ACT.Copy).then_inc(h_hi, 1)
                if phase:
                    act.wait_ge(g_ps, n + 1)
                    if at_least(n, 2):
                        act.wait_ge(h_ps, n - 1)
                    act.activation(hs[par], ps[:, 2 * par, :], ACT.Silu, scale=cgs[:, 0:1]).then_inc(silu, 1)
                if not (isinstance(n, int) and n + 1 >= NT):
                    x_hi(n + 1, 1 - par)
                if prev_phase == "slots":
                    r = n - (1 + NB)
                    act.wait_ge(y_ps, n)
                    act.wait_ge(meta, r + 1)
                    if at_least(r, 2):
                        act.wait_ge(y_out, r * 16 - 16)
                    w = mw[:, r:r + 1] if isinstance(r, int) else mw[:, ds(r, 1)]
                    act.activation(yb[1 - par], ps[:, 7 - par, 0:D], ACT.Identity, scale=w).then_inc(y_sb, 1)

            x_hi(0, 0)
            run_tiles(act, tile_act)

        @block.vector
        def _(dve):
            link = Chain(dve, dchain)
            dve.memset(neghalf, -0.5).then_inc(mset, 1)
            dve.memset(sc[:, 8:9], MAGIC)
            dve.memset(sc[:, 9:10], -MAGIC)
            dve.memset(rt8, 0.0)
            link(dve.memset(BD, 0.0))
            dve.memset(rt8[:, D + 1:D + 2], NO_ROW).then_inc(fill_ready, 1)

            def stats1(a, g, ch, between=None):
                if not (isinstance(g, int) and g == 0):
                    dve.wait_ge(a.xn, g)
                for b in range(GB):
                    last = dve.bn_stats(bnst[0][:, 6 * b:6 * b + 6], xt(g * GB + b))
                ch(last, mset)
                for b in range(GB):
                    last = dve.bn_aggr(mv[0][:, 2 * b:2 * b + 2], bnst[0][:, 6 * b:6 * b + 6])
                ch(last)
                dve.tensor_scalar(ve[0], mv[0].rearrange("p (b t) -> p t b", t=2)[:, 1, :], EPS, None, ALU.add).then_inc(a.ve1, 1)
                if between:
                    between()
                dve.wait_ge(a.rstd1, g + 1)
                dve.scalar_tensor_tensor(out=nmr, in0=mv[0].rearrange("p (b t) -> p t b", t=2)[:, 0, :], scalar=-1.0,
                                         in1=rs1, op0=ALU.mult, op1=ALU.mult).then_inc(a.nmr, 1)

            bv0 = rowv[:, R_BV0:R_BV0 + D].rearrange("p (a d) -> p a d", a=1).to_broadcast([P, GB, D])

            def evac_pv0(a, g):
                for h in range(2):
                    dve.wait_ge(a.pv_ps, 2 * g + h + 1)
                    if h == 0 and not (isinstance(g, int) and g == 0):
                        dve.wait_ge(a.res, g)
                    dve.tensor_tensor(otmp[:, 2 * h:2 * h + 2, :].rearrange("p b (j k) -> p (b j) k", k=64),
                                      pair(2 + h)[:, 0, :].rearrange("p (s k) -> p s k", k=64),
                                      rinv[:, 8 * h:8 * h + 8].rearrange("p (s a) -> p s a", a=1).to_broadcast([P, 8, 64]),
                                      ALU.mult).then_inc(a.pv, 1)

            def after0(a, g, ch):
                dve.wait_ge(a.res, g + 1)
                for b in range(GB):
                    last = dve.bn_stats(bnst[1][:, 6 * b:6 * b + 6], xt(g * GB + b))
                ch(last, mset)
                for b in range(GB):
                    last = dve.bn_aggr(mv[1][:, 2 * b:2 * b + 2], bnst[1][:, 6 * b:6 * b + 6])
                ch(last)
                if not (isinstance(g, int) and g == 0):
                    dve.wait_ge(a.rstd2, g)
                dve.tensor_scalar(ve[1], mv[1].rearrange("p (b t) -> p t b", t=2)[:, 1, :], EPS, None, ALU.add).then_inc(a.ve2, 1)

            def centre0(a, g):
                for b in range(GB):
                    last = dve.tensor_scalar(XN[:, ds(g * GB + b, 1), :].rearrange("p a d -> p (a d)") if not isinstance(g, int) else XN[:, g * GB + b, :],
                                             xt(g * GB + b), mv[1][:, 2 * b:2 * b + 1], None, ALU.subtract)
                last.then_inc(centred, 1)

            def max0(g):
                dve.wait_ge(centred, g + 1)
                gs = XN[:, ds(g * GB, GB), :] if not isinstance(g, int) else XN[:, g * GB:(g + 1) * GB, :]
                dve.tensor_reduce(xmx[:, ds(g * GB, GB)] if not isinstance(g, int) else xmx[:, g * GB:(g + 1) * GB],
                                  gs, AX.X, ALU.max).then_inc(xmx_done, 1)

            def weight_max(e):
                dve.wait_ge(wst_in, 16 * e + 16)
                o = wmx[:, 3 * e:3 * e + 3] if isinstance(e, int) else wmx[:, ds(e * 3, 3)]
                dve.tensor_reduce(o, wst.rearrange("p (m w) -> p m w", m=3), AX.X, ALU.max, apply_absolute_value=True).then_inc(wmax_done, 1)

            def evac_v0(a, g):
                dve.wait_ge(a.v_ps, g + 1)
                dve.tensor_tensor(v[:, :, :], pair(0).rearrange("p a (b d) -> p (a b) d", d=D), bv0, ALU.add).then_inc(a.v, 1)

            def attention0_dve(a, g, ch, has_prev, has_next2):
                if has_prev:
                    evac_pv0(a, g - 1)
                    evac_v0(a, g)
                after = (lambda: after0(a, g - 1, ch)) if has_prev else None
                if has_next2:
                    stats1(a, g + 2, ch, after)
                elif after:
                    after()
                dve.wait_ge(a.s_sb, 2 * g + 2)
                ch(dve.tensor_reduce(rmax, S[:, :, :], AX.X, ALU.max))
                dve.tensor_tensor(S[:, :, :], S[:, :, :], rmax.rearrange("p (s a) -> p s a", a=1).to_broadcast([P, 16, BLK]),
                                  ALU.subtract).then_inc(a.sub, 1)
                if has_prev:
                    centre0(a, g - 1)
                dve.wait_ge(a.exp, g + 1)
                ch(dve.tensor_reduce(rsum, S[:, :, :], AX.X, ALU.add))
                ch(dve.reciprocal(rinv, rsum))
                dve.tensor_scalar(rinv, rinv, tg[:, 0:1], None, ALU.mult)
                for c in range(4):
                    r = slice(BLK * c, BLK * (c + 1))
                    last = dve.transpose(BD[r, :, r], S[r, :, :])
                last.then_inc(a.pt, 1)
                if has_prev:
                    max0(g - 1)
                weight_max(g)

            def quantise_weights():
                dve.wait_ge(w12_in, 32)
                link(dve.tensor_reduce(sw1, w1f, AX.X, ALU.max, apply_absolute_value=True))
                link(dve.tensor_reduce(sw2, w2f, AX.X, ALU.max, apply_absolute_value=True))
                evac_v0(A0, 0)
                link(dve.tensor_scalar(sw1, sw1, QEPS, 1.0 / 127.0, ALU.max, ALU.mult))
                ins = dve.tensor_scalar(sw2, sw2, QEPS, 1.0 / 127.0, ALU.max, ALU.mult)
                ins.then_inc(sw2_sb, 1)
                dve.wait_ge(sw2_sb, 1)
                link(dve.reciprocal(iw1, sw1))
                link(dve.reciprocal(iw2, sw2))
                for f in range(FC):
                    last = dve.tensor_scalar(w1f[:, f, :], w1f[:, f, :], iw1[:, f:f + 1], MAGIC, ALU.mult, ALU.add)
                for c in range(2):
                    last = dve.tensor_scalar(w2f[:, c, :], w2f[:, c, :], iw2[:, c:c + 1], MAGIC, ALU.mult, ALU.add)
                link(last)
                dve.tensor_scalar(w1q, w1f, MAGIC, None, ALU.subtract)
                dve.tensor_scalar(w2q, w2f, MAGIC, None, ALU.subtract).then_inc(wq_ready, 1)

            a = A0
            CH0 = 7
            dve.wait_ge(x_in[0], 16)
            stats1(a, 0, link)
            dve.wait_ge(x_in[1], 16)
            stats1(a, 1, link)
            dve.wait_ge(c_in, 48)
            dve.wait_ge(tg_ready, 1)
            dve.tensor_copy(identb, ident)
            quantise_weights()
            dve.wait_ge(x_in[2], 16)
            attention0_dve(a, 0, link, False, True)
            with dve.Fori(1, NG - 2) as g:
                ch = Chain(dve, a.d, (g - 1) * CH0)
                attention0_dve(a, g, ch, True, True)
                assert ch.n == CH0, ch.n
            for g in (NG - 2, NG - 1):
                attention0_dve(a, g, link, True, False)
            evac_pv0(a, NG - 1)
            dve.wait_ge(a.pv, 2 * NG)
            dve.tensor_tensor(xg(NG - 1), xg(NG - 1), otmp, ALU.add).then_inc(a.res, 1)
            after0(a, NG - 1, link)
            centre0(a, NG - 1)
            max0(NG - 1)

            dve.wait_ge(a.rstd2, NG)
            dve.wait_ge(xmx_done, NG)
            link(dve.tensor_tensor(t32, xmx, rs2, ALU.mult))
            dve.tensor_reduce(g1[:, 0:1], t32, AX.X, ALU.max).then_inc(gm_ready, 1)
            dve.wait_ge(gm_all, 1)
            link(dve.tensor_scalar(sc[:, 0:1], g1[:, 1:2], QEPS, 1.0 / 255.0, ALU.max, ALU.mult))
            link(dve.reciprocal(sc[:, 1:2], sc[:, 0:1]))
            dve.tensor_scalar(aq, rs2, sc[:, 1:2], None, ALU.mult).then_inc(aq_ready, 1)
            link(dve.tensor_scalar(cf, sw1, sc[:, 0:1], None, ALU.mult))
            link(dve.reciprocal(tf, cf))
            link(dve.tensor_tensor(tf, tf, colv[:, C_B1:C_B1 + FC], ALU.mult))
            link(dve.tensor_scalar(tf, tf, MAGIC, MAGIC, ALU.add, ALU.subtract))
            link(dve.tensor_tensor(bf, tf, cf, ALU.mult))
            for w in range(2):
                dve.wait_ge(wT_ps, w + 1)
                dst, src = (w1T, psb[:, 0:2, :]) if w == 0 else (w2T, psb[:, 2:4, :])
                if w == 0:
                    dve.tensor_copy(dst, src).then_inc(wT_sb, 1)
                else:
                    dve.tensor_copy(dst.rearrange("p (a f) d -> p a (f d)", a=2), src).then_inc(wT_sb, 1)
            weight_max(E)
            dve.wait_ge(wmax_done, NE)
            dve.tensor_reduce(wm3, wmx.rearrange("p (e m) -> p m e", m=3), AX.X, ALU.max).then_inc(wm_ready, 1)

            def hidden_max(i):
                for half in range(2):
                    for q in range(4):
                        n = 4 * half + q
                        dve.wait_ge(fa_ps, i * 8 + n + 1)
                        gg = i * 2 + half
                        o = mxA[:, ds(gg, 1), 2 * q:2 * q + 2] if not isinstance(gg, int) else mxA[:, gg:gg + 1, 2 * q:2 * q + 2]
                        dve.tensor_reduce(o.rearrange("p a f -> p (a f)"), pair(n % 3), AX.X, ALU.max).then_inc(fa_max, 1)

            with dve.Fori(0, NG // 2) as i:
                hidden_max(i)
            dve.wait_ge(wm_all, 1)
            link(dve.tensor_scalar(wa3, wa3, 2.0 ** -30, None, ALU.max))
            link(dve.tensor_scalar(pw3.bitcast(I32), wa3.bitcast(I32), 0x7F800000, None, ALU.bitwise_and))
            link(dve.reciprocal(ip3, pw3))
            dve.tensor_scalar(cgs, pw3[:, 0:1], 2.0 ** -21, None, ALU.mult)
            dve.tensor_scalar(cus, ip3[:, 0:1], 2.0 ** -24, None, ALU.mult)
            link(dve.tensor_tensor(ysc, pw3[:, 0:1], pw3[:, 1:2], ALU.mult))
            link(dve.tensor_tensor(ysc, ysc, pw3[:, 2:3], ALU.mult))
            link(dve.tensor_scalar(ysc, ysc, 2.0 ** -10, tg[:, 3:4], ALU.mult, ALU.mult))
            dve.tensor_scalar(wsc, ip3, 2.0 ** 13, None, ALU.mult).then_inc(wsc_ready, 1)

            dve.wait_ge(fa_max, 4 * NG)
            link(dve.tensor_reduce(hm, mxA.rearrange("p g f -> p f g"), AX.X, ALU.max))
            link(dve.tensor_tensor(hm, hm, cf, ALU.mult))
            link(dve.tensor_tensor(hm, hm, bf, ALU.add))
            dve.tensor_reduce(g1[:, 2:3], hm, AX.X, ALU.max).then_inc(hm_ready, 1)
            dve.wait_ge(hm_all, 1)
            link(dve.tensor_scalar(sc[:, 2:3], g1[:, 3:4], QEPS, 1.0 / 255.0, ALU.max, ALU.mult))
            link(dve.reciprocal(sc[:, 3:4], sc[:, 2:3]))
            dve.tensor_scalar(ca, cf, sc[:, 3:4], None, ALU.mult)
            dve.tensor_scalar(ba, bf, sc[:, 3:4], None, ALU.mult).then_inc(cb_ready, 1)
            dve.wait_ge(swrow_in, 16)
            link(dve.tensor_scalar(trow.rearrange("p (c q) -> p c q", c=2), swrow.rearrange("p (q c) -> p c q", c=2),
                                   sc[:, 2:3], None, ALU.mult))
            link(dve.reciprocal(brow, trow))
            link(dve.tensor_tensor(brow, brow, rowv[:, R_B2:R_B2 + D], ALU.mult))
            link(dve.tensor_scalar(brow, brow, MAGIC, MAGIC, ALU.add, ALU.subtract))
            link(dve.scalar_tensor_tensor(out=brow, in0=brow, scalar=tg[:, 2:3], in1=trow, op0=ALU.mult, op1=ALU.mult))
            link(dve.tensor_scalar(crow, trow, tg[:, 2:3], None, ALU.mult))
            cb = crow.rearrange("p (a d) -> p a d", a=1).to_broadcast([P, GB, D])

            def split_lo(e):
                for m in range(3):
                    dve.wait_ge(whi, m + 1 if isinstance(e, int) and e == E else e * 3 + m + 4)
                    off = e * WEXP + m * MAT
                    hi = WM[:, ds(off, HALF)] if not isinstance(e, int) else WM[:, off:off + HALF]
                    lo = WM[:, ds(off + HALF, HALF)] if not isinstance(e, int) else WM[:, off + HALF:off + MAT]
                    last = dve.scalar_tensor_tensor(out=lo, in0=wst[:, m * HALF:(m + 1) * HALF], scalar=wsc[:, m:m + 1],
                                                    in1=hi, op0=ALU.mult, op1=ALU.subtract)
                last.then_inc(wlo, 1)

            def second_evac(g):
                dve.wait_ge(f2_ps, g + 1)
                if at_least(g, 1):
                    dve.wait_ge(f2_a, g)
                dve.tensor_tensor(otmp, pair(3).rearrange("p a (b d) -> p (a b) d", d=D), cb, ALU.mult).then_inc(f2_ev, 1)

            def hidden_round(i, first):
                for n in range(8):
                    dve.wait_ge(f1_act, i * 8 + n + 1)
                    q = n % 4
                    dve.tensor_scalar(hq[n // 4][:, 2 * q:2 * q + 2, :], hf[n % 2], MAGIC, MAGIC, ALU.add, ALU.subtract).then_inc(f1_q, 1)
                    if n == 6 or (n == 2 and not first):
                        second_evac(i * 2 + n // 4 - 1)

            hidden_round(0, True)
            split_lo(E)
            with dve.Fori(1, NG // 2) as i:
                hidden_round(i, False)
            dve.wait_ge(f2_res, 1)
            stats1(A1, 0, link)
            second_evac(NG - 1)

            bv1 = rowv[:, R_BV1:R_BV1 + D].rearrange("p (a d) -> p a d", a=1).to_broadcast([P, GB, D])

            def evac_pv1(a, g):
                dve.wait_ge(a.pv_ps, g + 1)
                dve.wait_ge(a.sub, g + 1)
                if at_least(g, 1):
                    dve.wait_ge(a.res, g)
                dve.tensor_tensor(B1.otmp, pair(3).rearrange("p a (b d) -> p (a b) d", d=D),
                                  rinv[:, 0:GB].rearrange("p (s a) -> p s a", a=1).to_broadcast([P, GB, D]), ALU.mult).then_inc(a.pv, 1)

            def after1(a, g, ch):
                dve.wait_ge(a.res, g + 1)
                for b in range(GB):
                    last = dve.bn_stats(bnst[1][:, 6 * b:6 * b + 6], xt(g * GB + b))
                ch(last, mset)
                for b in range(GB):
                    last = dve.bn_aggr(mv[1][:, 2 * b:2 * b + 2], bnst[1][:, 6 * b:6 * b + 6])
                ch(last)
                if at_least(g, 1):
                    dve.wait_ge(a.rstd2, g)
                mvt = mv[1].rearrange("p (b t) -> p t b", t=2)
                dve.tensor_scalar(ve[1], mvt[:, 1, :], EPS, None, ALU.add).then_inc(a.ve2, 1)
                o = mu4[:, ds(g * GB, GB)] if not isinstance(g, int) else mu4[:, g * GB:(g + 1) * GB]
                ch(dve.tensor_copy(o, mvt[:, 0, :]))

            def attention1_dve(a, g, ch, has_prev, has_next2):
                split_lo(g)
                if has_prev:
                    evac_pv1(a, g - 1)
                dve.wait_ge(a.v_ps, g + 1)
                dve.tensor_tensor(B1.v, pair(0).rearrange("p a (b d) -> p (a b) d", d=D), bv1, ALU.add).then_inc(a.v, 1)
                dve.wait_ge(a.s_ps, g + 1)
                dve.wait_ge(mneg, g + 1)
                if has_prev:
                    dve.wait_ge(a.pt_ps, g)
                dve.scalar_tensor_tensor(out=S1, in0=ps[:, 5, :].rearrange("p (b k) -> p b k", b=GB), scalar=1.0 / 16.0,
                                         in1=mk, op0=ALU.mult, op1=ALU.add).then_inc(a.s_sb, 1)
                dve.wait_ge(a.s_sb, g + 1)
                ch(dve.tensor_reduce(rmax[:, 0:GB], S1, AX.X, ALU.max))
                dve.tensor_scalar(negmax, rmax[:, 0:GB], -1.0, None, ALU.mult).then_inc(nmx, 1)
                after = (lambda: after1(a, g - 1, ch)) if has_prev else None
                if has_next2:
                    dve.wait_ge(f2_res, g + 3)
                    stats1(a, g + 2, ch, after)
                elif after:
                    after()
                dve.wait_ge(a.exp, g + 1)
                ch(dve.reciprocal(rinv[:, 0:GB], rsum[:, 0:GB]))
                dve.tensor_scalar(rinv[:, 0:GB], rinv[:, 0:GB], tg[:, 1:2], None, ALU.mult).then_inc(a.sub, 1)

            a = A1
            CH1 = 7
            dve.wait_ge(f2_res, 2)
            stats1(a, 1, link)
            attention1_dve(a, 0, link, False, True)
            with dve.Fori(1, NG - 2) as g:
                ch = Chain(dve, a.d, (g - 1) * CH1)
                attention1_dve(a, g, ch, True, True)
                assert ch.n == CH1, ch.n
            for g in (NG - 2, NG - 1):
                attention1_dve(a, g, link, True, False)

            def last_nmr(t0, t1):
                dve.wait_ge(a.rstd2, t1 // GB)
                dve.scalar_tensor_tensor(out=nm4[:, t0:t1], in0=mu4[:, t0:t1], scalar=-1.0, in1=rs2[:, t0:t1],
                                         op0=ALU.mult, op1=ALU.mult).then_inc(nm4_ready, 1)

            rb = rowv[:, R_RB:R_RB + E].rearrange("p (a e) -> p a e", a=1).to_broadcast([P, GB, E])

            def router_logits(g, par):
                dve.wait_ge(lg_ps, g + 1)
                lg_g = lg[:, g * GB * E:(g + 1) * GB * E] if isinstance(g, int) else lg[:, ds(g * GB * E, GB * E)]
                dve.tensor_tensor(lg_g.rearrange("p (b e) -> p b e", e=E),
                                  ps[:, 5 - par, 0:GB * E].rearrange("p (b e) -> p b e", e=E), rb, ALU.add).then_inc(lg_sb, 1)

            def router_copy(g, par):
                dve.wait_ge(xnb_ready, g + 1)
                rows_g = XR[:, g * GB:(g + 1) * GB, 0:D] if isinstance(g, int) else XR[:, ds(g * GB, GB), 0:D]
                dve.tensor_copy(rows_g, xnb[par]).then_inc(xr_copied, 1)

            last_nmr(0, NB - GB)
            evac_pv1(a, NG - 1)
            router_copy(0, 0)
            router_copy(1, 1)
            router_logits(0, 0)
            router_copy(2, 0)
            after1(a, NG - 1, link)
            router_logits(1, 1)
            router_copy(3, 1)
            last_nmr(NB - GB, NB)

            v3 = lambda z: z.rearrange("p (b e) -> p b e", e=E)
            oh = [rt[5], rt[6]]

            def choose(part, g0, g1):
                b, e = slice(g0 * GB, g1 * GB), slice(g0 * GB * E, g1 * GB * E)
                shape = [P, (g1 - g0) * GB, E]
                b3 = lambda z: z.rearrange("p (b a) -> p b a", a=1).to_broadcast(shape)
                index8 = cst[:, K_I8:K_I8 + E].rearrange("p (a e) -> p a e", a=1).to_broadcast(shape)
                pk = v3(pick[:, e])
                dve.wait_ge(sig, part)
                link(dve.tensor_scalar(lg[:, e], lg[:, e], 1.0, None, ALU.add))
                link(dve.reciprocal(lg[:, e], lg[:, e]))
                prob = [lg[:, e], left[:, e]]
                for k in range(2):
                    link(dve.tensor_reduce(mmax[k][:, b], v3(prob[k]), AX.X, ALU.max))
                    link(dve.tensor_tensor(pk, v3(prob[k]), b3(mmax[k][:, b]), ALU.is_ge))
                    link(dve.scalar_tensor_tensor(out=pk, in0=pk, scalar=-8.0, in1=index8, op0=ALU.mult, op1=ALU.add))
                    link(dve.tensor_reduce(imin[:, b], pk, AX.X, ALU.min))
                    link(dve.tensor_tensor(v3(oh[k][:, e]), pk, b3(imin[:, b]), ALU.is_equal))
                    if k == 0:
                        link(dve.scalar_tensor_tensor(out=prob[1], in0=oh[0][:, e], scalar=-4.0, in1=prob[0], op0=ALU.mult, op1=ALU.add))
                dve.tensor_tensor(rt[4][:, e], oh[0][:, e], oh[1][:, e], ALU.add).then_inc(oh_ready, 1)

            def router_step(i):
                router_logits(i * 2, 0)
                router_copy(i * 2 + 2, 0)
                router_logits(i * 2 + 1, 1)
                router_copy(i * 2 + 3, 1)

            with dve.Fori(1, NG // 2 - 1) as i:
                router_step(i)
            choose(1, 0, NG - 2)
            router_logits(NG - 2, 0)
            router_logits(NG - 1, 1)
            choose(2, NG - 2, NG)
            link(dve.tensor_tensor(wsum, mmax[0], mmax[1], ALU.add))
            link(dve.reciprocal(wsum, wsum))
            for k in range(2):
                dve.tensor_tensor(w12[k], mmax[k], wsum, ALU.mult)

            all_one = rt[7]
            link(dve.memset(all_one, 1.0))
            dve.wait_ge(rank_ps, 1)
            eb = lambda z: z.rearrange("p (b e) -> p e b", e=E)
            dve.tensor_copy(rt[1].rearrange("p (e b) -> p e b", e=E), eb(ps[:, 7, 0:NB * E]))
            dve.tensor_copy(rt[2], ps[:, 6, 0:NB * E]).then_inc(rank_sb, 1)
            dve.wait_ge(rank_sb, 1)
            exc = rt[3].rearrange("p (e b) -> p e b", e=E)
            cnt, til, inc, off, st = e8

            def tiles_of_experts():
                link(dve.tensor_tensor_scan(rt[0], all_one, rt[1], 0.0, ALU.mult, ALU.add))
                cum = rt[0].rearrange("p (e b) -> p e b", e=E)
                link(dve.tensor_tensor(rt[3], rt[0], rt[1], ALU.subtract))
                link(dve.tensor_tensor(cnt, cum[:, :, NB - 1], exc[:, :, 0], ALU.subtract))
                link(dve.tensor_scalar(til, cnt, 127.0, 1.0 / 128.0, ALU.add, ALU.mult))
                link(dve.tensor_scalar(til, til, 127.0 / 256.0, MAGIC, ALU.subtract, ALU.add))
                link(dve.tensor_scalar(til, til, MAGIC, None, ALU.subtract))
                link(dve.tensor_tensor_scan(inc, all_one[:, 0:E], til, 0.0, ALU.mult, ALU.add))
                link(dve.tensor_tensor(off, inc, til, ALU.subtract))
                link(dve.tensor_scalar(off, off, float(P), None, ALU.mult))
                link(dve.tensor_tensor(st, off, exc[:, :, 0], ALU.subtract))

            def slots_of(k):
                if k == 0:
                    link(dve.tensor_tensor(exc, exc, st.rearrange("p (e a) -> p e a", a=1).to_broadcast([P, E, NB]), ALU.add))
                    link(dve.tensor_tensor(v3(rt[1]), v3(rt[2]), rt[3].rearrange("p (e b) -> p b e", e=E), ALU.add))
                link(dve.tensor_tensor(rt[0], oh[k], rt[1], ALU.mult))
                link(dve.tensor_reduce(slotf[k], v3(rt[0]), AX.X, ALU.add))
                link(dve.tensor_copy(slot_i[k], slotf[k]))

            def experts_of_tiles():
                tl = work[:, 3 * 256:3 * 256 + RT * E].rearrange("p (t e) -> p t e", e=E)
                link(dve.tensor_tensor(tl, cst[:, K_TILE:K_TILE + RT].rearrange("p (t a) -> p t a", a=1).to_broadcast([P, RT, E]),
                                       inc.rearrange("p (a e) -> p a e", a=1).to_broadcast([P, RT, E]), ALU.is_ge))
                link(dve.tensor_reduce(rt[0][:, 0:RT], tl, AX.X, ALU.add))
                link(dve.tensor_scalar(eidx, rt[0][:, 0:RT], float(E - 1), float(WEXP), ALU.min, ALU.mult))
                dve.tensor_copy(XR[:, :, D + 1], cst[:, K_ROW:K_ROW + NB])
                dve.tensor_copy(XR[:, :, D], w12[0]).then_inc(slots_ready, 1)

            def x_lo(n, par):
                dve.wait_ge(t_hi, n + 1)
                if at_least(n, 2):
                    dve.wait_ge(u_ps, n - 1)
                dve.scalar_tensor_tensor(out=xl[par], in0=ps[:, 5, 0:D].rearrange("p (k t) -> p k t", k=KC), scalar=XSCALE,
                                         in1=xh[par], op0=ALU.mult, op1=ALU.subtract).then_inc(t_lo, 1)

            def slot_meta(n, par, loads):
                r = n - NB
                dve.wait_ge(xt_in[par], loads * 16)
                ow = mw[:, r:r + 1] if isinstance(r, int) else mw[:, ds(r, 1)]
                orow = mrow[:, r:r + 1] if isinstance(r, int) else mrow[:, ds(r, 1)]
                dve.tensor_scalar(ow, xt_[par][:, D:D + 1], ysc[:, 0:1], None, ALU.mult)
                dve.tensor_copy(orow, xt_[par][:, D + 1:D + 2]).then_inc(meta, 1)

            def tile_dve(i, par, phase, prev_phase):
                n = i * 2 + par
                if isinstance(n, int) and n == NB:
                    slot_meta(n, par, i + 1)
                if at_least(n, 1):
                    dve.wait_ge(h_hi, n)
                    if at_least(n, 3):
                        dve.wait_ge(y_ps, n - 2)
                    dve.tensor_tensor(hl[1 - par], ps[:, 4, :].rearrange("p (c t) -> p c t", c=IC), hh[1 - par], ALU.subtract).then_inc(h_lo, 1)
                if not (isinstance(n, int) and n + 1 >= NT):
                    x_lo(n + 1, 1 - par)
                if phase:
                    dve.wait_ge(u_ps, n + 1)
                    dve.wait_ge(silu, n + 1)
                    dve.scalar_tensor_tensor(out=hs[par], in0=ps[:, 2 * par + 1, :], scalar=cus[:, 0:1], in1=hs[par],
                                             op0=ALU.mult, op1=ALU.mult).then_inc(hid, 1)
                if phase == "slots" and not (isinstance(n, int) and n + 1 >= NT):
                    slot_meta(n + 1, 1 - par, i + par + 1)
                if prev_phase == "shared" and at_least(n, 1):
                    dve.wait_ge(y_ps, n)
                    z = xt(n - 1)
                    dve.scalar_tensor_tensor(out=z, in0=ps[:, 7 - par, 0:D], scalar=ysc[:, 0:1], in1=z,
                                             op0=ALU.mult, op1=ALU.add).then_inc(y_add, 1)

            def tile_and_routing(i, par, phase, prev_phase):
                tile_dve(i, par, phase, prev_phase)
                n = i * 2 + par
                if isinstance(n, int) and n < 4:
                    if n == 0:
                        tiles_of_experts()
                    elif n < 3:
                        slots_of(n - 1)
                    else:
                        experts_of_tiles()

            x_lo(0, 0)
            run_tiles(dve, tile_and_routing)

        @block.tensor
        def _(pe):
            def transposes(a, g, pr):
                pe.wait_ge(a.xn, g + 1)
                for b in range(GB):
                    for k in range(KC):
                        last = pe.transpose(pair(pr)[:, k, b * P:(b + 1) * P], a.B.xn[:, b, k * P:(k + 1) * P], ident)
                last.then_inc(a.xnT_ps, 1)

            def project_T(a, w, src, pr, done):
                for c in range(KC):
                    for k in range(KC):
                        last = pe.matmul(pair(pr)[:, c, :], watt[:, w, k, c * P:(c + 1) * P], src[:, k, :],
                                         start=(k == 0), stop=(k == KC - 1))
                last.then_inc(done, 1)

            def project_v(a, pr):
                for b in range(GB):
                    for k in range(KC):
                        last = pe.matmul(pair(pr)[:, b // 2, (b % 2) * D:(b % 2 + 1) * D], a.B.ctxb[:, k, b * P:(b + 1) * P],
                                         watt[:, 2, k, :], start=(k == 0), stop=(k == KC - 1))
                last.then_inc(a.v_ps, 1)

            def scores0(a, g):
                for h in range(2):
                    if at_least(g, 1):
                        pe.wait_ge(a.pv, 2 * g - 1 + h)
                    for s in range(8):
                        bb, jh, par = s // 4, (s // 2) % 2, s % 2
                        r = slice(64 * par, 64 * par + 64)
                        t = slice((2 * h + bb) * P, (2 * h + bb + 1) * P)
                        m = bb * 2 + jh
                        last = pe.matmul(pair(2 + h)[:, par, m * P:(m + 1) * P], qT[r, jh, t], kT[r, jh, t], start=True, stop=True)
                    last.then_inc(a.s_ps, 1)

            def attention0_pe(a, g, has_next):
                pe.wait_ge(a.xnT, g + 1)
                pe.wait_ge(a.v, g)
                project_T(a, 0, xnT, 0, a.q_ps)
                pe.wait_ge(ctx_in, 16 * g + 16)
                project_T(a, 1, ctxb, 1, a.k_ps)
                pe.wait_ge(a.q, g + 1)
                project_v(a, 0)
                pe.wait_ge(a.pt, g)
                for h in range(2):
                    for s in range(8):
                        b, j = 2 * h + s // NH0, s % NH0
                        last = pe.matmul(pair(2 + h)[:, 0, s * 64:(s + 1) * 64], BD[:, b * NH0 + j, :],
                                         v[:, b, j * 64:(j + 1) * 64], start=True, stop=True)
                    last.then_inc(a.pv_ps, 1)
                pe.wait_ge(a.k, g + 1)
                if has_next:
                    transposes(a, g + 1, 1)
                scores0(a, g)

            a = A0
            pe.wait_ge(wat_in, 16)
            pe.wait_ge(ctx_in, 16)
            project_T(a, 1, ctxb, 1, a.k_ps)
            project_v(a, 0)
            pe.wait_ge(c_in, 48)
            transposes(a, 0, 2)
            pe.wait_ge(a.xnT, 1)
            project_T(a, 0, xnT, 3, a.q_ps)
            pe.wait_ge(a.k, 1)
            transposes(a, 1, 1)
            pe.wait_ge(a.q, 1)
            scores0(a, 0)
            with pe.Fori(1, NG - 1) as g:
                attention0_pe(a, g, True)
            attention0_pe(a, NG - 1, False)
            pe.wait_ge(wq_ready, 1)
            pe.wait_ge(a.v, NG)
            for f in range(FC):
                for k in range(KC):
                    last = pe.transpose(psb[:, k, f * P:(f + 1) * P], w1q[:, f, k * P:(k + 1) * P], identb)
            last.then_inc(wT_ps, 1)
            pe.wait_ge(a.pt, NG)
            for h in range(2):
                for s in range(8):
                    b, j = 2 * h + s // NH0, s % NH0
                    last = pe.matmul(pair(2 + h)[:, 0, s * 64:(s + 1) * 64], BD[:, b * NH0 + j, :],
                                     v[:, b, j * 64:(j + 1) * 64], start=True, stop=True)
                last.then_inc(a.pv_ps, 1)
            pe.wait_ge(a.k, NG)
            for f in range(FC):
                for c in range(2):
                    last = pe.transpose(psb[:, 2 + f // 4, (f % 4) * D + c * P:(f % 4) * D + (c + 1) * P],
                                        w2q[:, c, f * P:(f + 1) * P], identb)
            last.then_inc(wT_ps, 1)

            def transposes_q(g):
                pe.wait_ge(xq_b, g + 1)
                if isinstance(g, int) and g == 0:
                    pe.wait_ge(a.pv, 2 * NG)
                else:
                    pe.wait_ge(xqT_sb, g)
                for b in range(GB):
                    for k in range(KC):
                        last = pe.transpose(psb[:, 7, k * GT + b * P:k * GT + (b + 1) * P], xqb[:, b, k * P:(k + 1) * P], identb)
                last.then_inc(xqT_ps, 1)

            def hidden(g, q, pr, done):
                for f in range(2):
                    for k in range(KC):
                        rhs = XQT[:, k, ds(g * GT, GT)] if not isinstance(g, int) else XQT[:, k, g * GT:(g + 1) * GT]
                        last = pe.matmul(pair(pr)[:, f, :], w1T[:, k, (2 * q + f) * P:(2 * q + f + 1) * P], rhs,
                                         start=(k == 0), stop=(k == KC - 1))
                last.then_inc(done, 1)

            def pass_a(i, first, last_pair):
                for half in range(2):
                    gg = i * 2 + half
                    if not (last_pair and half):
                        transposes_q(gg + 1)
                    pe.wait_ge(xqT_sb, gg + 1)
                    for q in range(4):
                        n = 4 * half + q
                        if n >= 3:
                            pe.wait_ge(fa_max, i * 8 + n - 2)
                        elif not first:
                            pe.wait_ge(fa_max, i * 8 + (-1, 0, -2)[n])
                        hidden(gg, q, n % 3, fa_ps)

            transposes_q(0)
            pe.wait_ge(wT_sb, 2)
            pass_a(0, True, False)
            with pe.Fori(1, NG // 2 - 1) as i:
                pass_a(i, False, False)
            pass_a(NG // 2 - 1, False, True)

            def second(g, half):
                pe.wait_ge(f1_q, g * 4 + 4)
                if at_least(g, 1):
                    pe.wait_ge(f2_ev, g)
                for b in range(GB):
                    for f in range(FC):
                        last = pe.matmul(pair(3)[:, b // 2, (b % 2) * D:(b % 2 + 1) * D],
                                         hq[half][:, f, b * P:(b + 1) * P], w2T[:, f, :], start=(f == 0), stop=(f == FC - 1))
                last.then_inc(f2_ps, 1)

            def pass_b(i, first):
                for n in range(8):
                    if n >= 3:
                        pe.wait_ge(f1_act, i * 8 + n - 2)
                    elif not first:
                        pe.wait_ge(f1_act, i * 8 + (-1, 0, -2)[n])
                    hidden(i * 2 + n // 4, n % 4, n % 3, f1_ps)
                    if n == 6 or (n == 2 and not first):
                        second(i * 2 + n // 4 - 1, 1 - n // 4)

            pe.wait_ge(fa_max, 4 * NG)
            pass_b(0, True)
            with pe.Fori(1, NG // 2) as i:
                pass_b(i, False)
            second(NG - 1, 1)

            def transpose_probs(a, g):
                pe.wait_ge(a.exp, g + 1)
                for b in range(GB):
                    last = pe.transpose(ps[:, 4, b * P:(b + 1) * P], S1[:, b, :], ident)
                last.then_inc(a.pt_ps, 1)

            def values(a, g):
                pe.wait_ge(a.pt, g + 1)
                if at_least(g, 1):
                    pe.wait_ge(a.pv, g)
                for b in range(GB):
                    last = pe.matmul(pair(3)[:, b // 2, (b % 2) * D:(b % 2 + 1) * D], PT[:, b, :], B1.v[:, b, :], start=True, stop=True)
                last.then_inc(a.pv_ps, 1)

            def attention1_pe(a, g, has_prev, has_next):
                pe.wait_ge(a.xnT, g + 1)
                if has_prev:
                    pe.wait_ge(a.v, g)
                project_T(a, 0, B1.xnT, 0, a.q_ps)
                pe.wait_ge(ctx1_in, 16 * g + 16)
                project_T(a, 1, B1.ctxb, 1, a.k_ps)
                pe.wait_ge(a.q, g + 1)
                project_v(a, 0)
                if has_prev:
                    transpose_probs(a, g - 1)
                    values(a, g - 1)
                pe.wait_ge(a.k, g + 1)
                if has_next:
                    transposes(a, g + 1, 1)
                if has_prev:
                    pe.wait_ge(a.s_sb, g)
                for b in range(GB):
                    for k in range(KC):
                        last = pe.matmul(ps[:, 5, b * P:(b + 1) * P], B1.qT[:, k, b * P:(b + 1) * P], B1.kT[:, k, b * P:(b + 1) * P],
                                         start=(k == 0), stop=(k == KC - 1))
                last.then_inc(a.s_ps, 1)

            a = A1
            pe.wait_ge(f1_act, 4 * NG)
            pe.wait_ge(wat_in, 32)
            transposes(a, 0, 1)
            attention1_pe(a, 0, False, True)
            pe.wait_ge(f2_ev, NG)
            with pe.Fori(1, NG - 1) as g:
                attention1_pe(a, g, True, True)
            attention1_pe(a, NG - 1, True, False)
            transpose_probs(a, NG - 1)
            values(a, NG - 1)

            pe.wait_ge(wrt_in, 16)
            pe.wait_ge(a.v, NG)

            def router_transposes(g, par):
                pe.wait_ge(xnb_ready, g + 1)
                if at_least(g, 2):
                    pe.wait_ge(xnbT_sb, g - 1)
                for b in range(GB):
                    for k in range(KC):
                        last = pe.transpose(pair(par)[:, k, b * P:(b + 1) * P], xnb[par][:, b, k * P:(k + 1) * P], ident)
                last.then_inc(xnbT_ps, 1)

            def router_products(g, par):
                pe.wait_ge(xnbT_sb, g + 1)
                if at_least(g, 2):
                    pe.wait_ge(lg_sb, g - 1)
                for b in range(GB):
                    for k in range(KC):
                        last = pe.matmul(ps[:, 5 - par, b * E:(b + 1) * E], xnbT[:, k, b * P:(b + 1) * P],
                                         wrts[:, k, :], start=(k == 0), stop=(k == KC - 1))
                last.then_inc(lg_ps, 1)

            pe.wait_ge(a.k, NG)
            pe.wait_ge(a.s_sb, NG)
            pe.wait_ge(a.pt, NG)
            router_transposes(0, 0)

            def router_pair(i):
                router_transposes(i * 2 + 1, 1)
                router_products(i * 2, 0)
                router_transposes(i * 2 + 2, 0)
                router_products(i * 2 + 1, 1)

            router_pair(0)
            with pe.Fori(1, NG // 2 - 1) as i:
                router_pair(i)
            router_transposes(NG - 1, 1)
            router_products(NG - 2, 0)
            router_products(NG - 1, 1)
            pe.wait_ge(oh_ready, 2)
            pe.matmul(ps[:, 6, 0:NB * E], tri, rt[4], start=True, stop=True)
            pe.matmul(ps[:, 7, 0:NB * E], ones, rt[4], start=True, stop=True).then_inc(rank_ps, 1)

            def x_transpose(n, par, loads):
                pe.wait_ge(xt_in[par], loads * 16)
                if at_least(n, 1):
                    pe.wait_ge(t_lo, n)
                for k in range(KC):
                    last = pe.transpose(ps[:, 5, k * P:(k + 1) * P], xt_[par][:, k * P:(k + 1) * P], ident)
                last.then_inc(t_ps, 1)

            def weights(phase, r, off, width):
                if phase != "slots":
                    return lambda o: WM[:, E * WEXP + off + o:E * WEXP + off + o + width]
                tile = eidx[0:1, r:r + 1] if isinstance(r, int) else eidx[0:1, ds(r, 1)]
                e = pe.value_load(tile, min_val=0, max_val=(E - 1) * WEXP)
                return lambda o: WM[:, ds(e + (off + o), width)]

            def tile_pe(i, par, phase, prev_phase):
                n = i * 2 + par
                if isinstance(n, int) and n == 1:
                    pe.wait_ge(rank_sb, 1)
                if isinstance(n, int) and n == NB:
                    pe.wait_ge(slots_ready, 1)
                w_up = weights(phase, n - NB, 0, I)
                if at_least(n, 1):
                    pe.wait_ge(hid, n)
                    if at_least(n, 2):
                        pe.wait_ge(h_lo, n - 1)
                    for c in range(IC):
                        last = pe.transpose(ps[:, 4, c * P:(c + 1) * P], hs[1 - par][:, c * P:(c + 1) * P], ident)
                    last.then_inc(h_ps, 1)
                last_tile = isinstance(n, int) and n + 1 >= NT
                if phase:
                    pe.wait_ge(t_hi, n + 1)
                    pe.wait_ge(t_lo, n + 1)
                    for m, done in ((0, g_ps), (1, u_ps)):
                        z = ps[:, 2 * par + m, :]
                        for k in range(KC):
                            pe.matmul(z, xh[par][:, k, :], w_up(m * MAT + k * I), start=(k == 0), stop=False)
                            pe.matmul(z, xh[par][:, k, :], w_up(m * MAT + HALF + k * I), start=False, stop=False)
                            last = pe.matmul(z, xl[par][:, k, :], w_up(m * MAT + k * I), start=False, stop=(k == KC - 1))
                        last.then_inc(done, 1)
                        if m == 0 and not last_tile:
                            x_transpose(n + 1, 1 - par, i + par + 1)
                w_down = weights(prev_phase, n - (1 + NB), 2 * MAT, D)
                if at_least(n, 1):
                    pe.wait_ge(h_hi, n)
                    pe.wait_ge(h_lo, n)
                    if at_least(n, 3):
                        if prev_phase == "shared" or (isinstance(n, int) and n < NB + 3):
                            pe.wait_ge(y_add, n - 2)
                        else:
                            pe.wait_ge(y_sb, n - (2 + NB))
                    z = ps[:, 7 - par, 0:D]
                    for c in range(IC):
                        pe.matmul(z, hh[1 - par][:, c, :], w_down(c * D), start=(c == 0), stop=False)
                        pe.matmul(z, hh[1 - par][:, c, :], w_down(HALF + c * D), start=False, stop=False)
                        last = pe.matmul(z, hl[1 - par][:, c, :], w_down(c * D), start=False, stop=(c == IC - 1))
                    last.then_inc(y_ps, 1)

            x_transpose(0, 0, 1)
            pe.wait_ge(wlo, NE)
            run_tiles(pe, tile_pe)


_IN = ["x", "ctxT", "mask", "wqkv0", "wqkv1", "cols", "rows", "w1", "w2", "wmoe", "wrt", "consts"]


def kernel(**inputs):
    import concourse.bacc as bacc
    from concourse.bass_utils import run_bass_kernel_spmd

    a = {k: np.asarray(v) for k, v in inputs.items()}
    seq = lambda z: z.reshape(NB, 32, 4, D).transpose(0, 2, 1, 3).reshape(NB, P, D)
    wmat = lambda w: w.reshape(KC, P, D).transpose(1, 0, 2)
    col = lambda z: z.reshape(-1, P).T
    ctxs = seq(a["ctx_1024"])
    m = a["mask_BxSxS2_fk0"].reshape(NB, 32, 4, 32, 4).transpose(2, 1, 0, 4, 3).reshape(P, NB, P)
    up = lambda w: w.reshape(I, KC, P).transpose(2, 1, 0).reshape(P, KC * I)
    down = lambda w: w.reshape(D, IC, P).transpose(2, 1, 0).reshape(P, IC * D)
    moe = [[up(w) for w in (*a["L1_ffn_wg"], a["L1_ffn_sg_w"])], [up(w) for w in (*a["L1_ffn_wu"], a["L1_ffn_su_w"])],
           [down(w) for w in (*a["L1_ffn_wd"], a["L1_ffn_sd_w"])]]
    data = {
        "x": seq(a["x"]).transpose(1, 0, 2),
        "ctxT": ctxs.reshape(NG, GT, KC, P).transpose(3, 0, 2, 1),
        "mask": m,
        "wqkv0": np.stack([wmat(a[f"L0_xattn_W{n}"].T) for n in "qkv"], 1),
        "wqkv1": np.stack([wmat(a[f"L1_xattn_W{n}"]) for n in "qkv"], 1),
        "cols": np.concatenate([col(a[n]) for n in ("L0_xattn_bq", "L0_xattn_bk", "L1_xattn_bq", "L1_xattn_bk", "L0_ffn_b1")], 1),
        "rows": np.concatenate([a[n].reshape(-1) for n in ("L0_xattn_bv", "L1_xattn_bv", "L0_ffn_b2", "L1_ffn_routing_bias", "g_xattn", "g_ffn")])[None],
        "w1": a["L0_ffn_w1"].reshape(FC, P, D).transpose(1, 0, 2),
        "w2": a["L0_ffn_w2"].reshape(2, P, F).transpose(1, 0, 2),
        "wmoe": np.stack([np.stack(w, 1) for w in moe], 2),
        "wrt": a["L1_ffn_router_w"].T.reshape(KC, P, E).transpose(1, 0, 2),
        "consts": np.concatenate([np.eye(P), np.triu(np.ones((P, P)), 1), np.ones((P, P)), np.tile(np.arange(E) + 8.0, (P, 1)),
                                  np.arange(P * NB).reshape(P, NB), np.tile(np.arange(RT), (P, 1))], 1).astype(np.float32),
    }
    nc = bacc.Bacc("TRN2", target_bir_lowering=False, num_devices=1)
    arrays, args = {}, []
    for n in _IN:
        z = np.ascontiguousarray(data[n])
        arrays[n] = z
        args.append(nc.dram_tensor(n, z.shape, F32, kind="ExternalInput").ap())
    args.append(nc.dram_tensor("result", (P, NB, D), F32, kind="ExternalOutput").ap())
    bass_gated_two_layer(nc, *args)
    r = run_bass_kernel_spmd(nc, [arrays], core_ids=[0])
    y = r.results[0]["result"]
    return y.reshape(4, 32, NB, D).transpose(2, 1, 0, 3).reshape(NB, P, D)
```
